# Optimizing a Trainium2 kernel written in Bass

```python
import numpy as np
import jax
import jax.numpy as jnp

def _softmax(x, axis=-1):
    return jax.nn.softmax(x, axis=axis)

def _gelu(x):
    return jax.nn.gelu(x, approximate=True)

def _silu(x):
    return jax.nn.silu(x)

def _sigmoid(x):
    return jax.nn.sigmoid(x)

def _layernorm(x, axis=-1, eps=1e-05):
    m = jnp.mean(x, axis=axis, keepdims=True)
    v = jnp.var(x, axis=axis, keepdims=True)
    return (x - m) / jnp.sqrt(v + eps)

def _scatter_add(tgt, idx, src, axis=0):
    return tgt.at[idx].add(src)

def _segment_sum(src, seg, n):
    return jax.ops.segment_sum(src, seg, n)
kernel_name = 'mk_adaln_d1_jaxref_r4_a59ed6'

def setup_inputs(seed: int=0):
    np.random.seed(seed)
    _w = jnp.asarray

    def _L0_attn_setup():
        import jax, jax.numpy as jnp
        import numpy as np
        import math
        D_MODEL = 512
        D_STATE = 16
        EXPAND = 2
        D_INNER = D_MODEL * EXPAND
        DT_RANK = math.ceil(D_MODEL / 16)
        BATCH, SEQ_LEN = (2, 128)
        key = jax.random.key(seed)
        ks = jax.random.split(key, 6)
        x = jax.random.normal(ks[0], (BATCH, SEQ_LEN, D_INNER), dtype=jnp.float32)
        A_log = jnp.log(jax.random.uniform(ks[1], (D_INNER, D_STATE), minval=0.5, maxval=16.0, dtype=jnp.float32))
        D = jnp.ones((D_INNER,), dtype=jnp.float32)
        x_proj_w = 0.02 * jax.random.normal(ks[2], (DT_RANK + 2 * D_STATE, D_INNER), dtype=jnp.float32)
        dt_init_std = DT_RANK ** (-0.5)
        dt_proj_w = jax.random.uniform(ks[3], (D_INNER, DT_RANK), minval=-dt_init_std, maxval=dt_init_std, dtype=jnp.float32)
        dt = jnp.exp(jax.random.uniform(ks[4], (D_INNER,), dtype=jnp.float32) * (math.log(0.1) - math.log(0.001)) + math.log(0.001))
        dt = jnp.clip(dt, 0.0001, None)
        dt_proj_b = dt + jnp.log(-jnp.expm1(-dt))
        return {'x': x, 'A_log': A_log, 'D': D, 'x_proj_w': x_proj_w, 'dt_proj_w': dt_proj_w, 'dt_proj_b': dt_proj_b}
    _L0_attn_in = _L0_attn_setup()

    def _L0_ffn_setup():
        import jax, jax.numpy as jnp
        import numpy as np
        D_MODEL = 1024
        D_HIDDEN = 2752
        RANK = 16
        BATCH, SEQ = (2, 512)

        def _matmul_lora(x, w, a, b, scale=1.0):
            out = jnp.einsum('bsd,hd->bsh', x, w)
            out = out + jnp.einsum('bsr,hr->bsh', jnp.einsum('bsd,rd->bsr', x, a), b) * scale
            return out
        key = jax.random.key(seed)
        ks = jax.random.split(key, 10)
        s = 0.02
        return {'x': jax.random.normal(ks[0], (BATCH, SEQ, D_MODEL), jnp.float32), 'gate_w': jax.random.normal(ks[1], (D_HIDDEN, D_MODEL), jnp.float32) * s, 'up_w': jax.random.normal(ks[2], (D_HIDDEN, D_MODEL), jnp.float32) * s, 'down_w': jax.random.normal(ks[3], (D_MODEL, D_HIDDEN), jnp.float32) * s, 'gate_a': jax.random.normal(ks[4], (RANK, D_MODEL), jnp.float32) * s, 'gate_b': jax.random.normal(ks[5], (D_HIDDEN, RANK), jnp.float32) * s, 'up_a': jax.random.normal(ks[6], (RANK, D_MODEL), jnp.float32) * s, 'up_b': jax.random.normal(ks[7], (D_HIDDEN, RANK), jnp.float32) * s, 'down_a': jax.random.normal(ks[8], (RANK, D_HIDDEN), jnp.float32) * s, 'down_b': jax.random.normal(ks[9], (D_MODEL, RANK), jnp.float32) * s}
    _L0_ffn_in = _L0_ffn_setup()
    _L0_c = _w((lambda *s: np.random.randn(*s).astype(np.float32) * 0.05)(1, 1024))
    _L0_wmod = _w((lambda *s: np.random.randn(*s).astype(np.float32) * 0.05)(1024, 6 * 1024) * 1024 ** (-0.5))
    _d = {'L0_attn_x': _L0_attn_in['x'], 'L0_attn_A_log': _L0_attn_in['A_log'], 'L0_attn_D': _L0_attn_in['D'], 'L0_attn_x_proj_w': _L0_attn_in['x_proj_w'], 'L0_attn_dt_proj_w': _L0_attn_in['dt_proj_w'], 'L0_attn_dt_proj_b': _L0_attn_in['dt_proj_b'], 'L0_ffn_gate_w': _L0_ffn_in['gate_w'], 'L0_ffn_up_w': _L0_ffn_in['up_w'], 'L0_ffn_down_w': _L0_ffn_in['down_w'], 'L0_ffn_gate_a': _L0_ffn_in['gate_a'], 'L0_ffn_gate_b': _L0_ffn_in['gate_b'], 'L0_ffn_up_a': _L0_ffn_in['up_a'], 'L0_ffn_up_b': _L0_ffn_in['up_b'], 'L0_ffn_down_a': _L0_ffn_in['down_a'], 'L0_ffn_down_b': _L0_ffn_in['down_b'], 'L0_c': _L0_c, 'L0_wmod': _L0_wmod}
    _x0 = _d['L0_attn_x']
    _d['L0_attn_x'] = jax.random.normal(jax.random.fold_in(jax.random.key(seed), 1), (1, 2048, 1024), dtype=_x0.dtype)
    del _x0
    return _d

def reference(L0_attn_x, L0_attn_A_log, L0_attn_D, L0_attn_x_proj_w, L0_attn_dt_proj_w, L0_attn_dt_proj_b, L0_ffn_gate_w, L0_ffn_up_w, L0_ffn_down_w, L0_ffn_gate_a, L0_ffn_gate_b, L0_ffn_up_a, L0_ffn_up_b, L0_ffn_down_a, L0_ffn_down_b, L0_c, L0_wmod):

    def _L0_attn_ref(x, A_log, D, x_proj_w, dt_proj_w, dt_proj_b):
        import jax, jax.numpy as jnp
        import numpy as np
        import math
        D_MODEL = 512
        D_STATE = 16
        EXPAND = 2
        D_INNER = D_MODEL * EXPAND
        DT_RANK = math.ceil(D_MODEL / 16)
        BATCH, SEQ_LEN = (2, 128)
        A = -jnp.exp(A_log)
        xp = jnp.einsum('bld,rd->blr', x, x_proj_w)
        dt_in = xp[..., :DT_RANK]
        B = xp[..., DT_RANK:DT_RANK + D_STATE]
        C = xp[..., DT_RANK + D_STATE:]
        dt = jax.nn.softplus(jnp.einsum('blr,dr->bld', dt_in, dt_proj_w) + dt_proj_b)
        dA = jnp.exp(dt[..., None] * A)
        dBx = dt[..., None] * B[:, :, None, :] * x[..., None]

        def step(h, inp):
            dA_t, dBx_t, C_t = inp
            h = dA_t * h + dBx_t
            y = jnp.einsum('bdn,bn->bd', h, C_t)
            return (h, y)
        h0 = jnp.zeros((x.shape[0], D_INNER, D_STATE), dtype=x.dtype)
        _, ys = jax.lax.scan(step, h0, (jnp.moveaxis(dA, 1, 0), jnp.moveaxis(dBx, 1, 0), jnp.moveaxis(C, 1, 0)))
        y = jnp.moveaxis(ys, 0, 1) + D * x
        return y

    def _L0_ffn_ref(x, gate_w, up_w, down_w, gate_a, gate_b, up_a, up_b, down_a, down_b):
        import jax, jax.numpy as jnp
        import numpy as np
        D_MODEL = 1024
        D_HIDDEN = 2752
        RANK = 16
        BATCH, SEQ = (2, 512)

        def _matmul_lora(x, w, a, b, scale=1.0):
            out = jnp.einsum('bsd,hd->bsh', x, w)
            out = out + jnp.einsum('bsr,hr->bsh', jnp.einsum('bsd,rd->bsr', x, a), b) * scale
            return out
        gate = _matmul_lora(x, gate_w, gate_a, gate_b)
        up = _matmul_lora(x, up_w, up_a, up_b)
        hidden = jax.nn.silu(gate) * up
        out = _matmul_lora(hidden, down_w, down_a, down_b)
        return out
    x = L0_attn_x
    mod = (_silu(L0_c) @ L0_wmod).reshape(L0_c.shape[0], 6, 1, -1)
    sa, ca, ga, sb, cb, gb = (mod[:, 0], mod[:, 1], mod[:, 2], mod[:, 3], mod[:, 4], mod[:, 5])
    ga = (2 * (ga >= 0) - 1) * jnp.maximum(jnp.abs(ga), 0.25)
    gb = (2 * (gb >= 0) - 1) * jnp.maximum(jnp.abs(gb), 0.25)
    h = _layernorm(x, axis=-1) * (1 + ca) + sa
    x = x + ga * _L0_attn_ref(h, L0_attn_A_log, L0_attn_D, L0_attn_x_proj_w, L0_attn_dt_proj_w, L0_attn_dt_proj_b)
    h = _layernorm(x, axis=-1) * (1 + cb) + sb
    x = x + gb * _L0_ffn_ref(h, L0_ffn_gate_w, L0_ffn_up_w, L0_ffn_down_w, L0_ffn_gate_a, L0_ffn_gate_b, L0_ffn_up_a, L0_ffn_up_b, L0_ffn_down_a, L0_ffn_down_b)
    return x

_drawn_inputs = setup_inputs


def setup_inputs(seed=0):
    import zlib

    import numpy as np

    out = dict(_drawn_inputs(seed))
    spreads = {'L0_attn_D': (1.0, 0.2)}
    factors = {'L0_attn_A_log': 4.636,
     'L0_attn_dt_proj_w': 6.554,
     'L0_attn_dt_proj_b': 3.41,
     'L0_ffn_gate_a': 8.0,
     'L0_ffn_gate_b': 8.0,
     'L0_ffn_up_a': 8.0,
     'L0_ffn_up_b': 8.0,
     'L0_ffn_down_a': 8.0,
     'L0_ffn_down_b': 8.0}
    for name, (base, spread) in spreads.items():
        noise = np.random.default_rng([zlib.crc32(name.encode()), seed]).standard_normal(out[name].shape)
        drawn = base * np.exp(spread * noise) if base else spread * noise
        out[name] = jnp.asarray(drawn.astype(out[name].dtype))
    for name, factor in factors.items():
        out[name] = (out[name] * factor).astype(out[name].dtype)
    return out
```

```python
from contextlib import ExitStack

import concourse.bass as bass
from concourse import mybir

ALU = mybir.AluOpType
ACT = mybir.ActivationFunctionType
F32 = mybir.dt.float32
F32R = mybir.dt.float32r

P = 128
D = 1024
ND = D // P
TOKENS = 2048
T = 512
CHUNKS = TOKENS // T
NS = 16
RANK = 32
HID = 2752
NH = -(-HID // P)
LORA = 16
LORA_AT = HID % P
EPS = 1e-5
PAIRS = ND // 2
GROUPS = NS * PAIRS
LOG1P = [0.9999999403953552, -0.4999949336051941, 0.3331909477710724, -0.24842961132526398,
         0.19105929136276245, -0.13663087785243988, 0.07822412997484207, -0.029504142701625824,
         0.005232425406575203]
MOD_ORDER = [1, 0, 2, 3, 4, 5]
CA, SA, GA, SB, CB, GB = range(6)
MOD_SLOTS = 16

PARTS = [(0, 8), (8, 15), (15, NH)]
PART_MAX = 8
UNITS = [("lora_a", 0, 0)]
for part, (k0, k1) in enumerate(PARTS):
    for j in range(k0, k1):
        UNITS += [("gate", part, j), ("up", part, j)]
    UNITS += [("lora_down", part, 0)] + [("down", part, m) for m in range(ND)]
NU = len(UNITS)
GU_COLS = (ND + 1) * P
LA_COLS = 2 * 2 * LORA
TD_COLS = LORA_AT + LORA
SLOT = GU_COLS
RAW_SLOTS, HI_SLOTS = 2, 3
AHEAD_SPLIT, AHEAD_LOAD = 2, 4
assert NU % RAW_SLOTS == 0 and NU % HI_SLOTS == 0 and NU % 2 == 0


def unit_at(*unit):
    return UNITS.index(unit)


def unit_cols(u):
    kind, part, _ = UNITS[u % NU]
    n = PARTS[part][1] - PARTS[part][0]
    return {"lora_a": ND * LA_COLS, "gate": GU_COLS, "up": GU_COLS, "lora_down": n * TD_COLS, "down": n * P}[kind]


PIECES = [(("sums", 0), 1), (("center", 0), 6), (("scale", 0), 9), (("project", 0), 7)]
PIECES += [(("dt", i), 13) for i in range(PAIRS)]
PIECES += [(("group", g), 3.6) for g in range(GROUPS)]
PIECES += [(("sums", 1), 1), (("center", 1), 6), (("scale", 1), 9)]
SCAN_UNITS = 68


def scan_at():
    total = sum(w for _, w in PIECES)
    at, done = [[] for _ in range(NU)], 0.0
    for piece, w in PIECES:
        at[min(NU - 1, int(done / total * SCAN_UNITS))].append(piece)
        done += w
    return at


SCAN_AT = scan_at()


def build(nc, x_c, mod_w, cT, ident, x_proj, dt_proj, dt_bias, a_log, d_vec, w_la, w_gu, w_td, w_dn, out_c):
    acc_dram = nc.dram_tensor("acc_scratch", (CHUNKS, P, ND, T), F32, kind="Internal").ap()

    with ExitStack() as ctx:
        def sb(name, shape, dt=F32, to=ctx):
            return to.enter_context(nc.sbuf_tensor(name, shape, dt))

        def sem(name):
            return ctx.enter_context(nc.semaphore(name))

        y = sb("y", [P, ND, T])
        hb = sb("hb", [P, ND, T])
        dtb = sb("dtb", [P, ND, T])
        ring = sb("ring", [P, 3, 2, T])
        xs = sb("xs", [P, T], F32R)
        xdt = sb("xdt", [RANK, T])
        hst = sb("hst", [P, NS * ND])
        sel = sb("sel", [P, 64], F32R)
        xpw = sb("xpw", [P, ND, P])
        dtw = sb("dtw", [RANK, D])
        ones = sb("ones", [P, P])
        vec = sb("vec", [P, 4, ND])
        aneg = sb("aneg", [P, ND * NS])
        mod = sb("mod", [P, 6, ND])
        gad = sb("gad", [P, ND])
        small = sb("small", [P, 2, ND])
        epsc = sb("epsc", [P, 1])
        identf = sb("identf", [P, 64])
        raw = sb("raw", [P, RAW_SLOTS, SLOT])
        whi = sb("whi", [P, HI_SLOTS, SLOT], F32R)
        wlo = sb("wlo", [P, HI_SLOTS, SLOT], F32R)
        ts = sb("ts", [LA_COLS, T], F32R)
        tda = sb("tda", [P, T])
        hid = sb("hid", [P, 2, T])
        pin = sb("pin", [P, 2, T])
        pout = sb("pout", [P, 2, T])
        with ExitStack() as early:
            modw = sb("modw", [P, MOD_SLOTS, ND, P], to=early)
        xhi = sb("xhi", [P, ND, T], F32R)
        xlo = sb("xlo", [P, ND, T], F32R)
        hhi = sb("hhi", [P, PART_MAX, T], F32R)
        hlo = sb("hlo", [P, PART_MAX, T], F32R)

        FP = ctx.enter_context(nc.psum_tensor("FP", [P, 2, T], F32))
        DA = ctx.enter_context(nc.psum_tensor("DA", [P, 2, T], F32))
        BB = ctx.enter_context(nc.psum_tensor("BB", [P, 2, T], F32))
        CC = ctx.enter_context(nc.psum_tensor("CC", [P, 2, T], F32))

        d_const, d_x, d_x2 = sem("const_loaded"), sem("x_loaded"), sem("x2_stored")
        d_modw = [sem(f"modw_loaded{s}") for s in range(MOD_SLOTS)]
        d_raw = [sem(f"raw_loaded{s}") for s in range(RAW_SLOTS)]
        d_pin = [sem(f"part_in_loaded{s}") for s in range(2)]
        d_pout = [sem(f"part_out_stored{s}") for s in range(2)]
        pe_sums, pe_xp, pe_dt, pe_bc = sem("sums_ready"), sem("xproj_ready"), sem("dt_raw_ready"), sem("bc_ready")
        pe_unit, pe_mod = sem("unit_done"), sem("mod_ready")
        a_step, a_sq, a_seed, a_h = sem("scalar_step"), sem("squares_ready"), sem("rsqrt_seed_ready"), sem("h_ready")
        a_h2, a_xs, a_sp = sem("h2_hi_ready"), sem("xs_rounded"), sem("softplus_parts_ready")
        a_da = [sem(f"decay{a}_ready") for a in range(2)]
        a_hi, a_th, a_hh, a_ls = sem("weight_hi_ready"), sem("tanh_ready"), sem("hidden_hi_ready"), sem("lora_rounded")
        a_const = sem("scalar_const_ready")
        v_const, v_step, v_mod = sem("vector_const_ready"), sem("vector_step"), sem("mod_vectors_ready")
        v_center, v_norm, v_xs, v_yinit = sem("centered"), sem("normed"), sem("xs_split"), sem("y_started")
        v_dt, v_dbx, v_hc, v_save = sem("dt_u_ready"), sem("dbx_ready"), sem("state_c_ready"), sem("state_kept")
        v_scan = [sem(f"scan{a}_done") for a in range(2)]
        v_used, v_c, v_hlo = sem("unit_used"), sem("silu_c_half"), sem("lora_lo_ready")
        g_lo, g_add, g_hlo, g_h2 = sem("weight_lo_ready"), sem("y_added"), sem("hidden_lo_ready"), sem("h2_lo_ready")

        N_CONST = 7 * 16
        N_HID = NH + 1
        tmp = [ring[:, 0, 0, :], ring[:, 0, 1, :], ring[:, 1, 0, :], ring[:, 1, 1, :]]

        def pair(t, q):
            return t[:, 2 * q:2 * q + 2, :]

        def over_pair(bank):
            return bank.unsqueeze(1).to_broadcast([P, 2, T])

        def used_by(c, n):
            return c * NU + n + 1

        def done_by(c, n):
            return c * NU + n + 1

        def split_by(c, n):
            return c * NH + n + 1

        def stored_by(c, n):
            return (c * 12 + n + 1) * 16

        def modc(which, i):
            return mod[:, which, i:i + 1]

        def down_seq(part, m):
            return m % 2, part * (ND // 2) + m // 2

        block = ctx.enter_context(nc.Block())

        @block.sync
        def _(sp):
            def load_raw(c, u):
                kind, part, j = UNITS[u % NU]
                k0, k1 = PARTS[part]
                src = {"lora_a": lambda: w_la, "gate": lambda: w_gu[j, 0], "up": lambda: w_gu[j, 1],
                       "lora_down": lambda: w_td[:, k0:k1, :], "down": lambda: w_dn[j, :, k0:k1, :]}[kind]()
                dst = raw[:, u % RAW_SLOTS, 0:unit_cols(u)]
                if len(src.shape) == 3:
                    dst = dst.rearrange("p (k m) -> p k m", k=k1 - k0)
                if c is not None:
                    sp.wait_ge(a_hi, c * NU + u - 1)
                    sp.wait_ge(g_lo, c * NU + u - 1)
                sp.dma_start(dst, src).then_inc(d_raw[u % RAW_SLOTS], 16)


            def store_x2(c):
                sp.wait_ge(g_add, (c + 1) * GROUPS)
                sp.dma_start(acc_dram[c], y[:, :, :]).then_inc(d_x2, 16)

            def load_x(c):
                sp.wait_ge(d_x2, c * 16)
                sp.wait_ge(v_center, 16 * c)
                sp.dma_start(y[:, :, :], x_c[c]).then_inc(d_x, 16)

            def load_part(c, part, m):
                s, k = down_seq(part, m)
                if m >= 2:
                    sp.wait_ge(v_used, used_by(c, unit_at("down", part, m - 2) + 1))
                elif part:
                    sp.wait_ge(v_used, used_by(c, unit_at("down", part - 1, m + ND - 2) + 1))
                else:
                    sp.wait_ge(v_used, used_by(c, 0))
                if part == 0:
                    sp.wait_ge(d_x2, (c + 1) * 16)
                else:
                    sp.wait_ge(d_pout[s], stored_by(c, k - 3))
                sp.dma_start(pin[:, s, :], acc_dram[c, :, m, :]).then_inc(d_pin[s], 16)

            def store_part(c, part, m):
                s, _ = down_seq(part, m)
                to = out_c if part == 2 else acc_dram
                sp.wait_ge(v_used, used_by(c, unit_at("down", part, m) + 1))
                sp.dma_start(to[c, :, m, :], pout[:, s, :]).then_inc(d_pout[s], 16)

            def units(c, scan):
                for u in range(NU):
                    if scan or u + AHEAD_LOAD < NU:
                        load_raw(c, u + AHEAD_LOAD)
                    kind, part, m = UNITS[u]
                    if kind == "down":
                        load_part(c, part, m)
                    if u >= 2 and UNITS[u - 2][0] == "down":
                        store_part(c, *UNITS[u - 2][1:])
                    if scan and ("sums", 1) in SCAN_AT[u]:
                        store_x2(c + 1)
                for u in (NU - 2, NU - 1):
                    store_part(c, *UNITS[u][1:])

            for s in range(2):
                sp.sem_inc(d_pout[s], 16)
            sp.dma_start(vec[:, 2, :], cT).then_inc(d_const, 16)
            sp.dma_start(y[:, :, :], x_c[0]).then_inc(d_x, 16)
            sp.dma_start(vec[:, 0, :], dt_bias).then_inc(d_const, 16)
            sp.dma_start(vec[:, 1, :], d_vec).then_inc(d_const, 16)
            sp.dma_start(aneg[:, :], a_log).then_inc(d_const, 16)
            sp.dma_start(identf[:, :], ident).then_inc(d_const, 16)
            sp.dma_start(xpw[:, :, :], x_proj).then_inc(d_const, 16)
            sp.dma_start(dtw[:, :], dt_proj).then_inc(d_const, 16)
            for n in range(6 * ND):
                if n >= MOD_SLOTS:
                    sp.wait_ge(pe_mod, n - MOD_SLOTS + 1)
                sp.dma_start(modw[:, n % MOD_SLOTS, :, :], mod_w[n]).then_inc(d_modw[n % MOD_SLOTS], 16)
                if n == MOD_SLOTS:
                    for u in range(RAW_SLOTS):
                        load_raw(None, u)
            for u in range(RAW_SLOTS, AHEAD_LOAD):
                load_raw(0, u)
            store_x2(0)
            with sp.Fori(0, CHUNKS - 1) as c:
                load_x(c + 1)
                units(c, True)
            units(CHUNKS - 1, False)
            sp.wait_ge(d_x2, CHUNKS * 16)
            for s in range(2):
                sp.wait_ge(d_pout[s], stored_by(CHUNKS, 0))

        @block.tensor
        def _(pe):
            def sums(c, k, of, bank):
                for i in range(ND):
                    last = nc.tensor.matmul(bank, ones[:, :], of[:, i, :], start=(i == 0), stop=(i == ND - 1))
                last.then_inc(pe_sums, 1)

            def scan_piece(c, kind, n):
                if kind == "sums":
                    if n == 0:
                        pe.wait_ge(d_x, (c + 1) * 16)
                    else:
                        pe.wait_ge(g_add, (c + 1) * GROUPS)
                        pe.wait_ge(v_hc, (c + 1) * GROUPS)
                    sums(c, n, y, BB[:, 0, :])
                elif kind == "scale":
                    pe.wait_ge(a_sq, 8 * c + 4 * n + 4)
                    sums(c, n, dtb, BB[:, 1, :])
                elif kind == "project":
                    pe.wait_ge(a_h, c + 1)
                    for i in range(ND):
                        last = nc.tensor.matmul(CC[:, 0, :], xpw[:, i, :], hb[:, i, :], start=(i == 0), stop=(i == ND - 1))
                    last.then_inc(pe_xp, 1)
                elif kind == "dt":
                    pe.wait_ge(a_xs, c + 1)
                    pe.wait_ge(a_sp, c * PAIRS + n)
                    for a in range(2):
                        i = 2 * n + a
                        last = nc.tensor.matmul(DA[:, a, :], dtw[:, i * P:(i + 1) * P], xdt[:, :], start=True, stop=True)
                    last.then_inc(pe_dt, 1)
                elif kind == "group" and n % PAIRS == 0:
                    s = n // PAIRS
                    if s == 0:
                        pe.wait_ge(v_xs, c + 1)
                    elif s >= 2:
                        pe.wait_ge(v_hc, c * GROUPS + PAIRS * (s - 1))
                    for bank, row in ((BB, RANK + s), (CC, RANK + NS + s)):
                        last = nc.tensor.matmul(bank[:, s % 2, :], sel[:, row:row + 1].to_broadcast([P, P]), xs[:, :],
                                                start=True, stop=True)
                    last.then_inc(pe_bc, 1)

            def products(out, pairs):
                n = len(pairs)
                for k, ((w_hi, w_lo), (x_hi, x_lo)) in enumerate(pairs):
                    for e, (w, x) in enumerate(((w_hi, x_hi), (w_hi, x_lo), (w_lo, x_hi))):
                        last = nc.tensor.matmul(out, w, x, start=(k == 0 and e == 0), stop=(k == n - 1 and e == 2))
                return last

            def unit(c, u):
                kind, part, j = UNITS[u]
                s, bank = u % HI_SLOTS, FP[:, u % 2, :]
                hi, lo = whi[:, s, :], wlo[:, s, :]
                k0, k1 = PARTS[part]
                pe.wait_ge(g_lo, c * NU + u + 1)
                pe.wait_ge(v_used, used_by(c, max(0, u - 1)))
                if kind == "lora_a":
                    pe.wait_ge(a_h2, c + 1)
                    pe.wait_ge(g_h2, c + 1)
                    last = products(FP[0:LA_COLS, u % 2, :], [
                        ((hi[:, k * LA_COLS:(k + 1) * LA_COLS], lo[:, k * LA_COLS:(k + 1) * LA_COLS]),
                         (xhi[:, k, :], xlo[:, k, :])) for k in range(ND)])
                elif kind in ("gate", "up"):
                    for k in range(ND):
                        at = slice(k * P, (k + 1) * P)
                        nc.tensor.matmul(bank, hi[:, at], xhi[:, k, :], start=(k == 0), stop=False)
                        nc.tensor.matmul(bank, hi[:, at], xlo[:, k, :], start=False, stop=False)
                        nc.tensor.matmul(bank, lo[:, at], xhi[:, k, :], start=False, stop=False)
                    if j == 0:
                        pe.wait_ge(v_used, used_by(c, 1))
                    nc.tensor.matmul(bank, lo[0:LA_COLS // 2, ND * P:], ts[0:LA_COLS // 2, :], start=False, stop=False)
                    last = nc.tensor.matmul(bank, hi[0:LA_COLS, ND * P:], ts[:, :], start=False, stop=True)
                else:
                    w = TD_COLS if kind == "lora_down" else P
                    n = k1 - k0
                    if kind == "lora_down":
                        pe.wait_ge(g_hlo, split_by(c, k1))
                    elif j == 0 and part == 2:
                        n -= 1
                    pairs = [((hi[:, k * w:(k + 1) * w], lo[:, k * w:(k + 1) * w]), (hhi[:, k, :], hlo[:, k, :]))
                             for k in range(k1 - k0)]
                    out = FP[0:w, u % 2, :]
                    if n == k1 - k0:
                        last = products(out, pairs)
                    else:
                        for k, ((w_hi, w_lo), (x_hi, x_lo)) in enumerate(pairs):
                            if k == n:
                                pe.wait_ge(v_hlo, c + 1)
                            for e, (a, b) in enumerate(((w_hi, x_hi), (w_hi, x_lo), (w_lo, x_hi))):
                                last = nc.tensor.matmul(out, a, b, start=(k == 0 and e == 0), stop=(k == n and e == 2))
                last.then_inc(pe_unit, 1)

            def mods(a, b):
                for n in range(a, b):
                    pe.wait_ge(d_modw[n % MOD_SLOTS], (n // MOD_SLOTS + 1) * 16)
                    col = FP[:, n // (3 * ND), n % (3 * ND):n % (3 * ND) + 1]
                    for k in range(ND):
                        last = nc.tensor.matmul(col, modw[:, n % MOD_SLOTS, k, :], vec[:, 3, k:k + 1],
                                                start=(k == 0), stop=(k == ND - 1))
                    last.then_inc(pe_mod, 1)

            pe.sem_inc(pe_unit, 1)
            pe.wait_ge(v_const, 2)
            pe.wait_ge(d_const, N_CONST)
            pe.wait_ge(a_const, 3)
            for kind, n in [p for p, _ in PIECES]:
                if (kind, n) == ("project", 0):
                    mods(0, 3 * ND)
                if (kind, n) == ("group", 2 * PAIRS):
                    mods(3 * ND, 6 * ND)
                scan_piece(0, kind, n)
            pe.wait_ge(v_mod, 2)
            with pe.Fori(0, CHUNKS - 1) as c:
                for u in range(NU):
                    for kind, n in SCAN_AT[u]:
                        scan_piece(c + 1, kind, n)
                    unit(c, u)
            for u in range(NU):
                unit(CHUNKS - 1, u)

        @block.scalar
        def _(act):
            PER = 2 * 2 + PAIRS + 1

            def scan_piece(c, kind, n):
                if kind == "center":
                    for q in range(PAIRS):
                        act.wait_ge(v_center, (2 * c + n) * 8 + 2 * q + 2)
                        nc.scalar.activation(pair(dtb, q), pair(hb, q), ACT.Square).then_inc(a_sq, 1)
                elif kind == "scale":
                    at = c * PER + (2 + PAIRS) * n
                    act.wait_ge(pe_sums, 4 * c + 2 * n + 2)
                    nc.scalar.activation(tmp[0], BB[:, 1, :], ACT.Ln, scale=1.0 / D, bias=epsc[:, :]).then_inc(a_step, 1)
                    act.wait_ge(a_step, at + 1)
                    nc.scalar.activation(tmp[1], tmp[0], ACT.Exp, scale=-0.5).then_inc(a_step, 1)
                    act.wait_ge(a_step, at + 2)
                    nc.scalar.activation(tmp[2], tmp[1], ACT.Square).then_inc(a_seed, 1)
                    if n == 0:
                        if isinstance(c, int) and c == 0:
                            act.wait_ge(v_mod, 1)
                        for i in range(ND):
                            if i % 2 == 0:
                                act.wait_ge(v_norm, 8 * c + i // 2 + 1)
                            last = nc.scalar.activation(hb[:, i, :], hb[:, i, :], ACT.Identity, scale=modc(CA, i), bias=modc(SA, i))
                        last.then_inc(a_h, 1)
                    else:
                        if isinstance(c, int) and c == 0:
                            act.wait_ge(v_mod, 2)
                        else:
                            act.wait_ge(pe_unit, done_by(c - 1, LAST_UP + 1))
                        for i in range(ND):
                            if i % 2 == 0:
                                act.wait_ge(v_norm, 8 * c + 4 + i // 2 + 1)
                            last = nc.scalar.activation(xhi[:, i, :], hb[:, i, :], ACT.Identity, scale=modc(CB, i), bias=modc(SB, i))
                        last.then_inc(a_step, 1)
                        act.wait_ge(a_step, at + 3)
                        for i in range(ND):
                            last = nc.scalar.activation(hb[:, i, :], hb[:, i, :], ACT.Identity, scale=modc(CB, i), bias=modc(SB, i))
                        last.then_inc(a_h2, 1)
                elif kind == "project":
                    act.wait_ge(pe_xp, c + 1)
                    if not (isinstance(c, int) and c == 0):
                        act.wait_ge(pe_bc, c * NS)
                        act.wait_ge(pe_dt, c * PAIRS)
                    nc.scalar.activation(xs[:, :], CC[:, 0, :], ACT.Copy)
                    nc.scalar.activation(xdt[:, :], CC[0:RANK, 0, :], ACT.Copy).then_inc(a_xs, 1)
                elif kind == "dt":
                    act.wait_ge(pe_dt, c * PAIRS + n + 1)
                    if n >= 2:
                        act.wait_ge(v_dt, c * PAIRS + n - 1)
                    for a in range(2):
                        i = 2 * n + a
                        nc.scalar.activation(ring[:, n % 2, a, :], DA[:, a, :], ACT.Abs, bias=vec[:, 0, i:i + 1])
                        e = nc.scalar.activation(dtb[:, i, :], DA[:, a, :], ACT.Relu, bias=vec[:, 0, i:i + 1])
                    e.then_inc(a_step, 1)
                    act.wait_ge(a_step, c * PER + 2 + n + 1)
                    nc.scalar.activation(ring[:, n % 2, :, :], ring[:, n % 2, :, :], ACT.Exp, scale=-1.0).then_inc(a_sp, 1)
                elif kind == "group":
                    s, q = divmod(n, PAIRS)
                    if s == 0:
                        act.wait_ge(v_dt, c * PAIRS + q + 1)
                    for a in range(2):
                        i = 2 * q + a
                        act.wait_ge(v_scan[a], c * GROUPS + n)
                        nc.scalar.activation(DA[:, a, :], dtb[:, i, :], ACT.Exp,
                                             scale=aneg[:, i * NS + s:i * NS + s + 1]).then_inc(a_da[a], 1)

            def split_hi(c, u, first=False):
                s, r, w = u % HI_SLOTS, u % RAW_SLOTS, unit_cols(u)
                act.wait_ge(d_raw[r], 16 * (c * (NU // RAW_SLOTS) + u // RAW_SLOTS + 1))
                if not first:
                    act.wait_ge(pe_unit, done_by(c, max(0, u - HI_SLOTS + 1)))
                nc.scalar.activation(whi[:, s, 0:w], raw[:, r, 0:w], ACT.Copy).then_inc(a_hi, 1)

            def before(c, u):
                kind, part, j = UNITS[u - 1]
                bank = (u - 1) % 2
                if kind == "lora_a":
                    act.wait_ge(pe_unit, done_by(c, u))
                    nc.scalar.activation(ts[:, :], FP[0:LA_COLS, bank, :], ACT.Copy).then_inc(a_ls, 1)
                elif kind == "gate":
                    act.wait_ge(pe_unit, done_by(c, u))
                    act.wait_ge(g_hlo, split_by(c, max(0, j - 1)))
                    nc.scalar.activation(hid[:, j % 2, :], FP[:, bank, :], ACT.Tanh, scale=0.5).then_inc(a_th, 1)

            def after(c, u):
                kind, part, j = UNITS[u - 1]
                if kind == "up":
                    act.wait_ge(v_used, used_by(c, u))
                    nc.scalar.activation(hhi[:, j - PARTS[part][0], :], hid[:, j % 2, :], ACT.Copy).then_inc(a_hh, 1)
                elif kind == "lora_down" and part == 2:
                    act.wait_ge(v_used, used_by(c, u))
                    at = slice(LORA_AT, LORA_AT + LORA)
                    nc.scalar.activation(hhi[at, NH - 1 - PARTS[2][0], :], hid[at, NH % 2, :], ACT.Copy).then_inc(a_hh, 1)

            act.wait_ge(d_const, N_CONST)
            act.wait_ge(v_const, 1)
            nc.scalar.activation(small[:, 0, :], vec[:, 2, :], ACT.Tanh, scale=0.5).then_inc(a_const, 1)
            nc.scalar.activation(aneg[:, :], aneg[:, :], ACT.Exp).then_inc(a_const, 1)
            nc.scalar.activation(sel[:, :], identf[:, :], ACT.Copy).then_inc(a_const, 1)
            for kind, n in [p for p, _ in PIECES]:
                scan_piece(0, kind, n)
                if (kind, n) == ("group", 3 * PAIRS):
                    for u in range(AHEAD_SPLIT):
                        split_hi(0, u, first=True)
            with act.Fori(0, CHUNKS - 1) as c:
                for u in range(NU):
                    if u:
                        before(c, u)
                    split_hi(c, u + AHEAD_SPLIT)
                    for kind, n in SCAN_AT[u]:
                        scan_piece(c + 1, kind, n)
                    if u:
                        after(c, u)
            for u in range(NU):
                if u:
                    before(CHUNKS - 1, u)
                if u + AHEAD_SPLIT < NU:
                    split_hi(CHUNKS - 1, u + AHEAD_SPLIT)
                if u:
                    after(CHUNKS - 1, u)

        @block.vector
        def _(dve):
            PER = 2 * 3 + PAIRS * (len(LOG1P) + 1)
            V = nc.vector

            def dbx(c, g):
                s, q = divmod(g, PAIRS)
                if q == 0:
                    dve.wait_ge(pe_bc, c * NS + s + 1)
                if g >= 3:
                    dve.wait_ge(g_add, c * GROUPS + g - 2)
                V.tensor_tensor(ring[:, g % 3, :, :], pair(hb, q), over_pair(BB[:, s % 2, :]), ALU.mult).then_inc(v_dbx, 1)

            def scan_piece(c, kind, n):
                if kind == "center":
                    dve.wait_ge(pe_sums, 4 * c + 2 * n + 1)
                    if n == 0 and not (isinstance(c, int) and c == 0):
                        dve.wait_ge(g_h2, c)
                    for q in range(PAIRS):
                        V.scalar_tensor_tensor(out=pair(hb, q), in0=over_pair(BB[:, 0, :]), scalar=-1.0 / D,
                                               in1=pair(y, q), op0=ALU.mult, op1=ALU.add).then_inc(v_center, 2)
                elif kind == "scale":
                    at = c * PER + (3 + PAIRS * (len(LOG1P) + 1)) * n
                    dve.wait_ge(a_seed, 2 * c + n + 1)
                    V.tensor_scalar(tmp[3], BB[:, 1, :], 1.0 / D, EPS, ALU.mult, ALU.add).then_inc(v_step, 1)
                    dve.wait_ge(v_step, at + 1)
                    V.scalar_tensor_tensor(out=tmp[3], in0=tmp[3], scalar=-0.5, in1=tmp[2], op0=ALU.mult, op1=ALU.mult).then_inc(v_step, 1)
                    dve.wait_ge(v_step, at + 2)
                    V.scalar_tensor_tensor(out=tmp[0], in0=tmp[3], scalar=1.5, in1=tmp[1], op0=ALU.add, op1=ALU.mult).then_inc(v_step, 1)
                    dve.wait_ge(v_step, at + 3)
                    for q in range(PAIRS):
                        V.tensor_tensor(pair(hb, q), pair(hb, q), over_pair(tmp[0]), ALU.mult).then_inc(v_norm, 1)
                elif kind == "project":
                    dve.wait_ge(a_h, c + 1)
                    for i in range(ND):
                        last = V.scalar_tensor_tensor(out=y[:, i, :], in0=hb[:, i, :], scalar=gad[:, i:i + 1], in1=y[:, i, :],
                                                      op0=ALU.mult, op1=ALU.add)
                    last.then_inc(v_yinit, 1)
                    dve.wait_ge(a_xs, c + 1)
                    V.tensor_tensor(xs[64:128, :], CC[64:128, 0, :], xs[64:128, :].bitcast(F32), ALU.subtract).then_inc(v_xs, 1)
                elif kind == "dt":
                    at = c * PER + 3 + n * (len(LOG1P) + 1)
                    dve.wait_ge(a_sp, c * PAIRS + n + 1)
                    e, poly = ring[:, n % 2, :, :], ring[:, 2, :, :]
                    V.tensor_scalar(poly, e, LOG1P[-1], None, ALU.mult).then_inc(v_step, 1)
                    for k, coefficient in enumerate(LOG1P[-2::-1]):
                        dve.wait_ge(v_step, at + k + 1)
                        V.scalar_tensor_tensor(out=poly, in0=poly, scalar=coefficient, in1=e, op0=ALU.add, op1=ALU.mult).then_inc(v_step, 1)
                    dve.wait_ge(v_step, at + len(LOG1P))
                    V.tensor_tensor(pair(dtb, n), pair(dtb, n), poly, ALU.add).then_inc(v_step, 1)
                    dve.wait_ge(v_step, at + len(LOG1P) + 1)
                    if n == 0:
                        dve.wait_ge(v_yinit, c + 1)
                    for i in (2 * n, 2 * n + 1):
                        last = V.scalar_tensor_tensor(out=hb[:, i, :], in0=dtb[:, i, :], scalar=modc(GA, i), in1=hb[:, i, :],
                                                      op0=ALU.mult, op1=ALU.mult)
                    last.then_inc(v_dt, 1)
                elif kind == "group":
                    s, q = divmod(n, PAIRS)
                    if n == 0:
                        dve.wait_ge(v_dt, (c + 1) * PAIRS)
                        dbx(c, 0)
                    buf = ring[:, n % 3, :, :]
                    dve.wait_ge(v_dbx, c * GROUPS + n + 1)
                    for a in range(2):
                        i = 2 * q + a
                        dve.wait_ge(a_da[a], c * GROUPS + n + 1)
                        initial = 0.0 if isinstance(c, int) and c == 0 else hst[:, s * ND + i:s * ND + i + 1]
                        V.tensor_tensor_scan(buf[:, a, :], DA[:, a, :], buf[:, a, :], initial, ALU.mult, ALU.add).then_inc(v_scan[a], 1)
                    if n + 1 < GROUPS:
                        dbx(c, n + 1)
                    for a in range(2):
                        dve.wait_ge(v_scan[a], c * GROUPS + n + 1)
                    V.tensor_copy(hst[:, s * ND + 2 * q:s * ND + 2 * q + 2], buf[:, :, T - 1]).then_inc(v_save, 1)
                    dve.wait_ge(v_save, c * GROUPS + n + 1)
                    V.tensor_tensor(buf, buf, over_pair(CC[:, s % 2, :]), ALU.mult).then_inc(v_hc, 1)

            def used(c, u):
                kind, part, j = UNITS[u - 1]
                bank = (u - 1) % 2
                h = hid[:, j % 2, :]
                if kind == "lora_a":
                    dve.wait_ge(a_ls, c + 1)
                    V.tensor_tensor(ts[32:64, :], FP[32:64, bank, :], ts[32:64, :].bitcast(F32), ALU.subtract).then_inc(v_used, 1)
                elif kind == "gate":
                    dve.wait_ge(a_th, c * NH + j + 1)
                    V.scalar_tensor_tensor(out=h, in0=h, scalar=1.0, in1=FP[:, bank, :], op0=ALU.add, op1=ALU.mult).then_inc(v_used, 1)
                elif kind == "up":
                    dve.wait_ge(pe_unit, done_by(c, u))
                    dve.wait_ge(v_used, used_by(c, u - 1))
                    V.scalar_tensor_tensor(out=h, in0=h, scalar=0.5, in1=FP[:, bank, :], op0=ALU.mult, op1=ALU.mult).then_inc(v_used, 1)
                elif kind == "lora_down":
                    at = slice(LORA_AT, LORA_AT + LORA)
                    dve.wait_ge(pe_unit, done_by(c, u))
                    if part == 0:
                        V.tensor_copy(tda[at, :], FP[at, bank, :]).then_inc(v_used, 1)
                    elif part == 1:
                        V.tensor_tensor(tda[at, :], FP[at, bank, :], tda[at, :], ALU.add).then_inc(v_used, 1)
                    else:
                        dve.wait_ge(g_hlo, split_by(c, NH - 1))
                        V.tensor_tensor(hid[at, NH % 2, :], FP[at, bank, :], tda[at, :], ALU.add).then_inc(v_used, 1)
                else:
                    if (part, j) == (2, 0):
                        dve.wait_ge(a_hh, (c + 1) * N_HID)
                        at, k = slice(LORA_AT, LORA_AT + LORA), NH - 1 - PARTS[2][0]
                        V.tensor_tensor(hlo[at, k, :], hid[at, NH % 2, :], hhi[at, k, :].bitcast(F32), ALU.subtract).then_inc(v_hlo, 1)
                    s, k = down_seq(part, j)
                    dve.wait_ge(pe_unit, done_by(c, u))
                    dve.wait_ge(d_pin[s], (c * 12 + k + 1) * 16)
                    dve.wait_ge(d_pout[s], stored_by(c, k))
                    V.scalar_tensor_tensor(out=pout[:, s, :], in0=FP[:, bank, :], scalar=modc(GB, j), in1=pin[:, s, :],
                                           op0=ALU.mult, op1=ALU.add).then_inc(v_used, 1)

            def mod_vectors():
                n = [0]

                def then(ins):
                    n[0] += 1
                    ins.then_inc(v_const, 1)
                    dve.wait_ge(v_const, 2 + n[0])

                def away_from_zero(v):
                    then(V.tensor_scalar(small[:, 0, :], v, 0.0, 2.0, ALU.is_ge, ALU.mult))
                    then(V.scalar_tensor_tensor(out=small[:, 1, :], in0=v, scalar=-1.0, in1=v, op0=ALU.mult, op1=ALU.max))
                    then(V.tensor_scalar(small[:, 1, :], small[:, 1, :], 0.25, None, ALU.max))
                    then(V.scalar_tensor_tensor(out=v, in0=small[:, 0, :], scalar=-1.0, in1=small[:, 1, :], op0=ALU.add, op1=ALU.mult))

                def first():
                    dve.wait_ge(pe_mod, 3 * ND)
                    then(V.tensor_copy(mod[:, 0:3, :], FP[:, 0, 0:3 * ND].rearrange("p (a b) -> p a b", a=3)))
                    then(V.tensor_scalar(mod[:, CA, :], mod[:, CA, :], 1.0, None, ALU.add))
                    away_from_zero(mod[:, GA, :])
                    dve.wait_ge(a_const, 2)
                    then(V.tensor_scalar(aneg[:, :], aneg[:, :], -1.0, None, ALU.mult))
                    V.tensor_tensor(gad[:, :], mod[:, GA, :], vec[:, 1, :], ALU.mult).then_inc(v_mod, 1)
                    dve.wait_ge(v_mod, 1)

                def second():
                    dve.wait_ge(pe_mod, 6 * ND)
                    then(V.tensor_copy(mod[:, 3:6, :], FP[:, 1, 0:3 * ND].rearrange("p (a b) -> p a b", a=3)))
                    then(V.tensor_scalar(mod[:, CB, :], mod[:, CB, :], 1.0, None, ALU.add))
                    away_from_zero(mod[:, GB, :])
                    V.tensor_copy(small[:, 0, :], mod[:, GB, :]).then_inc(v_mod, 1)
                return first, second

            dve.sem_inc(v_used, 1)
            V.memset(ones[:, :], 1.0)
            V.memset(epsc[:, :], EPS).then_inc(v_const, 1)
            dve.wait_ge(d_const, N_CONST)
            dve.wait_ge(a_const, 1)
            V.scalar_tensor_tensor(out=small[:, 0, :], in0=small[:, 0, :], scalar=1.0, in1=vec[:, 2, :],
                                   op0=ALU.add, op1=ALU.mult).then_inc(v_c, 1)
            dve.wait_ge(v_c, 1)
            V.tensor_scalar(vec[:, 3, :], small[:, 0, :], 0.5, None, ALU.mult).then_inc(v_const, 1)
            mod_first, mod_second = mod_vectors()
            for kind, n in [p for p, _ in PIECES]:
                if (kind, n) == ("project", 0):
                    mod_first()
                scan_piece(0, kind, n)
                if (kind, n) == ("group", 3 * PAIRS):
                    mod_second()
            with dve.Fori(0, CHUNKS - 1) as c:
                for u in range(NU):
                    if u:
                        used(c, u)
                    for kind, n in SCAN_AT[u]:
                        scan_piece(c + 1, kind, n)
                used(c, NU)
            for u in range(1, NU + 1):
                used(CHUNKS - 1, u)

        @block.gpsimd
        def _(pool):
            G = nc.gpsimd

            def scan_piece(c, kind, n):
                if kind == "group":
                    q = n % PAIRS
                    pool.wait_ge(v_hc, c * GROUPS + n + 1)
                    if n >= PAIRS:
                        pool.wait_ge(g_add, c * GROUPS + n - PAIRS + 1)
                    G.tensor_tensor(pair(y, q), pair(y, q), ring[:, n % 3, :, :], ALU.add).then_inc(g_add, 1)
                elif kind == "scale" and n == 1:
                    pool.wait_ge(a_h2, c + 1)
                    for q in range(PAIRS):
                        last = G.tensor_tensor(pair(xlo, q), pair(hb, q), pair(xhi, q).bitcast(F32), ALU.subtract)
                    last.then_inc(g_h2, 1)

            def split_lo(c, u):
                s, r, w = u % HI_SLOTS, u % RAW_SLOTS, unit_cols(u)
                pool.wait_ge(a_hi, c * NU + u + 1)
                G.tensor_tensor(wlo[:, s, 0:w], raw[:, r, 0:w], whi[:, s, 0:w].bitcast(F32), ALU.subtract).then_inc(g_lo, 1)

            def after(c, u):
                kind, part, j = UNITS[u - 1]
                if kind == "up":
                    pool.wait_ge(a_hh, c * N_HID + j + 1)
                    k = j - PARTS[part][0]
                    G.tensor_tensor(hlo[:, k, :], hid[:, j % 2, :], hhi[:, k, :].bitcast(F32), ALU.subtract).then_inc(g_hlo, 1)

            pool.sem_inc(g_hlo, 1)
            for kind, n in [p for p, _ in PIECES]:
                scan_piece(0, kind, n)
                if (kind, n) == ("group", 3 * PAIRS):
                    for u in range(AHEAD_SPLIT):
                        split_lo(0, u)
            with pool.Fori(0, CHUNKS - 1) as c:
                for u in range(NU):
                    split_lo(c, u + AHEAD_SPLIT)
                    for kind, n in SCAN_AT[u]:
                        scan_piece(c + 1, kind, n)
                    if u:
                        after(c, u)
            for u in range(NU):
                if u + AHEAD_SPLIT < NU:
                    split_lo(CHUNKS - 1, u + AHEAD_SPLIT)
                if u:
                    after(CHUNKS - 1, u)


LAST_UP = max(u for u, unit in enumerate(UNITS) if unit[0] == "up")


def layout(L0_attn_x, L0_attn_A_log, L0_attn_D, L0_attn_x_proj_w, L0_attn_dt_proj_w, L0_attn_dt_proj_b,
           L0_ffn_gate_w, L0_ffn_up_w, L0_ffn_down_w, L0_ffn_gate_a, L0_ffn_gate_b, L0_ffn_up_a, L0_ffn_up_b,
           L0_ffn_down_a, L0_ffn_down_b, L0_c, L0_wmod):
    import numpy as np

    def columns(v):
        return v.reshape(ND, P).T

    def blocks(w, rows):
        padded = np.zeros((rows, w.shape[1]), w.dtype)
        padded[:w.shape[0]] = w
        return padded.reshape(rows, w.shape[1] // P, P).transpose(2, 1, 0)

    f = np.float32
    wm = L0_wmod.reshape(ND, P, 6, ND, P)[:, :, MOD_ORDER].transpose(2, 3, 1, 0, 4).reshape(6 * ND, P, ND, P)
    xp = np.concatenate([blocks(L0_attn_x_proj_w, 64)] * 2, axis=2)
    w_la = np.concatenate([blocks(L0_ffn_gate_a, LORA), blocks(L0_ffn_up_a, LORA)] * 2, axis=2).reshape(P, ND * LA_COLS)
    w_gu = np.zeros((NH, 2, P, ND + 1, P), f)
    for n, (w, b) in enumerate(((L0_ffn_gate_w, L0_ffn_gate_b), (L0_ffn_up_w, L0_ffn_up_b))):
        w_gu[:, n, :, 0:ND, :] = blocks(w, NH * P).reshape(P, ND, NH, P).transpose(2, 0, 1, 3)
        padded = np.zeros((NH * P, LORA), f)
        padded[:HID] = b
        b_rows = padded.reshape(NH, P, LORA).transpose(0, 2, 1)
        for r in range(2):
            at = r * 2 * LORA + n * LORA
            w_gu[:, n, at:at + LORA, ND, :] = b_rows
    down = np.zeros((D, NH * P), f)
    down[:, :HID] = L0_ffn_down_w
    down[:, HID:HID + LORA] = L0_ffn_down_b
    w_dn = down.reshape(ND, P, NH, P).transpose(0, 3, 2, 1)
    down_a = np.zeros((TD_COLS, NH * P), f)
    down_a[LORA_AT:, :HID] = L0_ffn_down_a
    w_td = down_a.reshape(TD_COLS, NH, P).transpose(2, 1, 0)
    return {
        "x_c": L0_attn_x[0].reshape(CHUNKS, T, ND, P).transpose(0, 3, 2, 1), "mod_w": wm, "cT": columns(L0_c[0]), "ident": np.concatenate([np.eye(64, dtype=f)] * 2),
        "x_proj": xp, "dt_proj": L0_attn_dt_proj_w.T, "dt_bias": columns(L0_attn_dt_proj_b),
        "a_log": L0_attn_A_log.reshape(ND, P, NS).transpose(1, 0, 2).reshape(P, ND * NS), "d_vec": columns(L0_attn_D),
        "w_la": w_la, "w_gu": w_gu.reshape(NH, 2, P, GU_COLS), "w_td": w_td, "w_dn": w_dn,
    }


def kernel(**inputs):
    import numpy as np
    import concourse.bacc as bacc
    from concourse.bass_utils import run_bass_kernel_spmd

    nc = bacc.Bacc("TRN2", target_bir_lowering=False, num_devices=1)
    arrays = {n: np.ascontiguousarray(a) for n, a in layout(**{k: np.asarray(v) for k, v in inputs.items()}).items()}
    args = {n: nc.dram_tensor(n, a.shape, F32, kind="ExternalInput").ap() for n, a in arrays.items()}
    out_c = nc.dram_tensor("out_c", (CHUNKS, P, ND, T), F32, kind="ExternalOutput").ap()
    build(nc, **args, out_c=out_c)
    r = run_bass_kernel_spmd(nc, [arrays], core_ids=[0])
    return np.ascontiguousarray(r.results[0]["out_c"].transpose(0, 3, 2, 1)).reshape(1, TOKENS, D)
```

```python
from contextlib import ExitStack

import concourse.bass as bass
from concourse import mybir

ALU = mybir.AluOpType
ACT = mybir.ActivationFunctionType
F32 = mybir.dt.float32
F32R = mybir.dt.float32r

P = 128
D = 1024
ND = D // P
TOKENS = 2048
T = 512
CHUNKS = TOKENS // T
NS = 16
RANK = 32
HID = 2752
NH = -(-HID // P)
LORA = 16
LORA_AT = HID % P
EPS = 1e-5
PAIRS = ND // 2
GROUPS = NS * PAIRS
POOL_GROUPS = list(range(3, GROUPS - 4, 4))
LOG1P = [0.9999999403953552, -0.4999949336051941, 0.3331909477710724, -0.24842961132526398,
         0.19105929136276245, -0.13663087785243988, 0.07822412997484207, -0.029504142701625824,
         0.005232425406575203]
MOD_ORDER = [1, 0, 2, 3, 4, 5]
CA, SA, GA, SB, CB, GB = range(6)
MOD_SLOTS = 16
MOD_BEFORE_PREP = 3 * ND + MOD_SLOTS

PARTS = [(0, 7), (7, 14), (14, NH)]
PART_MAX = 8
UNITS = [("lora_a", 0, 0)]
for part, (k0, k1) in enumerate(PARTS):
    for j in range(k0 + (part > 0), min(k1 + 1, NH)):
        UNITS += [("gate", part, j), ("up", part, j)]
    UNITS += [("lora_down", part, 0)] + [("down", part, m) for m in range(ND)]
NU = len(UNITS)
GU_COLS = (ND + 1) * P
LA_COLS = 2 * 2 * LORA
TD_COLS = LORA_AT + LORA
SLOT = GU_COLS
RAW_SLOTS, HI_SLOTS = 2, 3
AHEAD_SPLIT, AHEAD_LOAD = 2, 3
BANKS = 4
STAGES = 3
PER_STAGE = len(PARTS) * ND // STAGES
assert PER_STAGE * STAGES == len(PARTS) * ND
assert NU % RAW_SLOTS == 0 and NU % HI_SLOTS == 0 and NU % BANKS == 0


def unit_at(*unit):
    return UNITS.index(unit)


def unit_cols(u):
    kind, part, _ = UNITS[u % NU]
    n = PARTS[part][1] - PARTS[part][0]
    return {"lora_a": ND * LA_COLS, "gate": GU_COLS, "up": GU_COLS, "lora_down": n * TD_COLS, "down": n * P}[kind]


POLY = 3
PIECES = []


def norm_pieces(n):
    at = [(n * PAIRS + q) for q in range(PAIRS)]
    return ([((None, 0), 11 * n), (("sums", n), 0.1), ((None, 0), 8)] + [(("center", k), 1.3) for k in at] + [((None, 0), 6), (("squares", n), 0.1)]
            + [((None, 0), 8), (("rstd", n), 4)] + [(("norm", k), 1.3) for k in at])


PIECES += norm_pieces(0)
PIECES += [((None, 0), 4), (("start", 0), 2.5), (("start", 1), 2.5), (("project", 0), 0.1), ((None, 0), 9), (("split", 0), 1), (("dt", 0), 1)]
for q in range(PAIRS):
    PIECES += [(("poly", q * POLY + k), 3.7) for k in range(POLY)]
    if q + 1 < PAIRS:
        PIECES += [(("dt", q + 1), 0.1)]
    PIECES += [(("u", q), 2.6)]
for g in range(GROUPS):
    PIECES += [(("states", g), 1.3), (("group", g), 2.5)]
PIECES += norm_pieces(1) + [(("h2", q), 0.5) for q in range(PAIRS)]


SCAN_SHARE = 0.985


def unit_passes(u):
    kind, part, _ = UNITS[u]
    n = PARTS[part][1] - PARTS[part][0]
    return {"lora_a": 3 * ND, "gate": 3 * ND + 2, "up": 3 * ND + 2}.get(kind, 3 * n)


def scan_at():
    total, passes = sum(w for _, w in PIECES), sum(unit_passes(u) for u in range(NU))
    at, done, u, ended = [[] for _ in range(NU)], 0.0, 0, unit_passes(0)
    for piece, w in PIECES:
        while u + 1 < NU and done / total * SCAN_SHARE * passes >= ended:
            u += 1
            ended += unit_passes(u)
        if piece[0] is not None:
            at[u].append(piece)
        done += w
    return at


SCAN_AT = scan_at()
FIRST_GROUP_UNIT = next(u for u, pieces in enumerate(SCAN_AT) if ("group", 0) in pieces)
CACHED = list(range(FIRST_GROUP_UNIT + 2, FIRST_GROUP_UNIT + 2 + 2 * 22, 2))
NC = len(CACHED)
PREP_AT = {}
for i in range(NC):
    PREP_AT.setdefault(("dt", i // 3) if i < 3 * PAIRS else ("group", 3 * (i - 3 * PAIRS)), []).append(i)
START_AT = ("group", 10 * PAIRS)


def made_before(u):
    return u - sum(k < u for k in CACHED)


def cached_before(u, s):
    return sum(k < u and k % HI_SLOTS == s for k in CACHED)


PIECES_ALONE = [piece for piece, _ in PIECES if piece[0] is not None]


def build(nc, x_c, mod_w, cT, ident, x_proj, dt_proj, dt_bias, a_log, d_vec, w_la, w_gu, w_td, w_dn, out_c):
    lo_dram = nc.dram_tensor("lo_scratch", (NC, P, SLOT), F32, kind="Internal").ap()
    acc_dram = nc.dram_tensor("acc_scratch", (CHUNKS, P, ND, T), F32, kind="Internal").ap()

    with ExitStack() as ctx:
        def sb(name, shape, dt=F32, to=ctx):
            return to.enter_context(nc.sbuf_tensor(name, shape, dt))

        def sem(name):
            return ctx.enter_context(nc.semaphore(name))

        y = sb("y", [P, ND, T])
        hb = sb("hb", [P, ND, T])
        dtb = sb("dtb", [P, ND, T])
        ring = sb("ring", [P, 3, 2, T])
        xs = sb("xs", [P, T], F32R)
        xdt = sb("xdt", [RANK, T])
        b_row = sb("b_row", [P, 2, T])
        c_row = sb("c_row", [P, 2, T])
        hst = sb("hst", [P, NS * ND])
        sel = sb("sel", [P, 64], F32R)
        xpw = sb("xpw", [P, ND, P])
        dtw = sb("dtw", [RANK, D])
        ones = sb("ones", [P, P])
        vec = sb("vec", [P, 4, ND])
        aneg = sb("aneg", [P, ND * NS])
        mod = sb("mod", [P, 6, ND])
        gad = sb("gad", [P, ND])
        small = sb("small", [P, 2, ND])
        epsc = sb("epsc", [P, 1])
        identf = sb("identf", [P, 64])
        raw = sb("raw", [P, RAW_SLOTS, SLOT])
        whi = sb("whi", [P, HI_SLOTS, SLOT], F32R)
        wlo = sb("wlo", [P, HI_SLOTS, SLOT], F32R)
        ts = sb("ts", [LA_COLS, T], F32R)
        tda = sb("tda", [P, T])
        hid = sb("hid", [P, 2, T])
        pin = sb("pin", [P, STAGES, T])
        pout = sb("pout", [P, STAGES, T])
        with ExitStack() as early:
            modw = sb("modw", [P, MOD_SLOTS, ND, P], to=early)
        xhi = sb("xhi", [P, ND, T], F32R)
        xlo = sb("xlo", [P, ND, T], F32R)
        hhi = sb("hhi", [P, PART_MAX, T], F32R)
        hlo = sb("hlo", [P, PART_MAX, T], F32R)

        FP = ctx.enter_context(nc.psum_tensor("FP", [P, BANKS, T], F32))
        DA = ctx.enter_context(nc.psum_tensor("DA", [P, 2, T], F32))
        BC = ctx.enter_context(nc.psum_tensor("BC", [P, 2, T], F32))

        d_const, d_x, d_x2 = sem("const_loaded"), sem("x_loaded"), sem("x2_stored")
        d_modw = [sem(f"modw_loaded{s}") for s in range(MOD_SLOTS)]
        d_prep = [sem(f"prep_loaded{s}") for s in range(RAW_SLOTS)]
        d_prep_out = [sem(f"prep_stored{s}") for s in range(HI_SLOTS)]
        d_lo = [sem(f"weight_lo_loaded{s}") for s in range(HI_SLOTS)]
        d_raw = [sem(f"raw_loaded{s}") for s in range(RAW_SLOTS)]
        d_pin = [sem(f"part_in_loaded{s}") for s in range(STAGES)]
        d_pout = [sem(f"part_out_stored{s}") for s in range(STAGES)]
        pe_sums, pe_xp, pe_dt, pe_bc = sem("sums_ready"), sem("xproj_ready"), sem("dt_raw_ready"), sem("bc_ready")
        pe_unit, pe_mod = sem("unit_done"), sem("mod_ready")
        a_step, a_sq, a_seed, a_h = sem("scalar_step"), sem("squares_ready"), sem("rsqrt_seed_ready"), sem("h_ready")
        a_h2, a_xs, a_sp = sem("h2_hi_ready"), sem("xs_rounded"), sem("softplus_parts_ready")
        a_da = [sem(f"decay{a}_ready") for a in range(2)]
        a_hi, a_th, a_hh, a_ls = sem("weight_hi_ready"), sem("tanh_ready"), sem("hidden_hi_ready"), sem("lora_rounded")
        g_hc, a_bc = sem("state_c_ready_by_gpsimd"), sem("bc_copied")
        a_prep, g_prep = sem("prep_hi_ready"), sem("prep_lo_ready")
        a_const = sem("scalar_const_ready")
        v_const, v_step, v_mod = sem("vector_const_ready"), sem("vector_step"), sem("mod_vectors_ready")
        v_center, v_norm, v_xs, v_yinit = sem("centered"), sem("normed"), sem("xs_split"), sem("y_started")
        v_dt, v_dbx, v_hc, v_save = sem("dt_u_ready"), sem("dbx_ready"), sem("state_c_ready"), sem("state_kept")
        v_scan = [sem(f"scan{a}_done") for a in range(2)]
        v_used, v_c, v_hlo = sem("unit_used"), sem("silu_c_half"), sem("lora_lo_ready")
        g_lo, g_add, g_hlo, g_h2 = sem("weight_lo_ready"), sem("y_added"), sem("hidden_lo_ready"), sem("h2_lo_ready")

        N_CONST = 7 * 16
        N_HID = NH + 1
        tmp = [ring[:, 0, 0, :], ring[:, 0, 1, :], ring[:, 1, 0, :], ring[:, 1, 1, :]]

        def pair(t, q):
            return t[:, 2 * q:2 * q + 2, :]

        def over_pair(bank):
            return bank.unsqueeze(1).to_broadcast([P, 2, T])

        def used_by(c, n):
            return c * NU + n + 1

        def done_by(c, n):
            return c * NU + n + 1

        def split_by(c, n):
            return c * NH + n + 1

        def stored_by(c, n):
            return (c * PER_STAGE + n + 1) * 16

        def lo_made(c, u):
            return c * (NU - NC) + made_before(u)

        def lo_loaded(c, u):
            s = u % HI_SLOTS
            return (c * cached_before(NU, s) + cached_before(u, s) + 1) * 16

        def modc(which, i):
            return mod[:, which, i:i + 1]

        def down_seq(part, m):
            n = part * ND + m
            return n % STAGES, n // STAGES

        def load_mod(engine, n):
            if n >= MOD_SLOTS:
                engine.wait_ge(pe_mod, n - MOD_SLOTS + 1)
            engine.dma_start(modw[:, n % MOD_SLOTS, :, :], mod_w[n]).then_inc(d_modw[n % MOD_SLOTS], 16)

        block = ctx.enter_context(nc.Block())

        @block.sync
        def _(sp):
            def load_raw(c, u):
                src, dst = unit_weights(u)
                if c is not None:
                    if u - RAW_SLOTS in CACHED:
                        sp.wait_ge(a_hi, c * NU + u - 1)
                    else:
                        sp.wait_ge(g_lo, lo_made(c, u - 1))
                sp.dma_start(dst, src).then_inc(d_raw[u % RAW_SLOTS], 16)

            def load_lo(c, u):
                s, w = u % HI_SLOTS, unit_cols(u)
                sp.wait_ge(pe_unit, done_by(c, u - HI_SLOTS + 1))
                sp.dma_start(wlo[:, s, 0:w].bitcast(F32), lo_dram[CACHED.index(u), :, 0:w]).then_inc(d_lo[s], 16)

            def unit_weights(u):
                kind, part, j = UNITS[u % NU]
                k0, k1 = PARTS[part]
                src = {"lora_a": lambda: w_la, "gate": lambda: w_gu[j, 0], "up": lambda: w_gu[j, 1],
                       "lora_down": lambda: w_td[:, k0:k1, :], "down": lambda: w_dn[j, :, k0:k1, :]}[kind]()
                dst = raw[:, u % RAW_SLOTS, 0:unit_cols(u)]
                return src, dst if len(src.shape) == 2 else dst.rearrange("p (k m) -> p k m", k=k1 - k0)

            def load_prep(i):
                if i >= RAW_SLOTS:
                    sp.wait_ge(g_prep, i - RAW_SLOTS + 1)
                src, dst = unit_weights(CACHED[i])
                into = raw[:, i % RAW_SLOTS, 0:unit_cols(CACHED[i])]
                into = into if len(dst.shape) == 2 else into.rearrange("p (k m) -> p k m", k=dst.shape[1])
                sp.dma_start(into, src).then_inc(d_prep[i % RAW_SLOTS], 16)

            def store_prep(i):
                w = unit_cols(CACHED[i])
                sp.wait_ge(g_prep, i + 1)
                sp.dma_start(lo_dram[i, :, 0:w], wlo[:, i % HI_SLOTS, 0:w].bitcast(F32)).then_inc(d_prep_out[i % HI_SLOTS], 16)

            def store_x2(c):
                sp.wait_ge(g_add, (c + 1) * GROUPS)
                sp.dma_start(acc_dram[c], y[:, :, :]).then_inc(d_x2, 16)

            def load_x(c):
                sp.wait_ge(d_x2, c * 16)
                sp.wait_ge(v_center, 16 * c)
                sp.dma_start(y[:, :, :], x_c[c]).then_inc(d_x, 16)

            def load_part(c, part, m):
                n = part * ND + m
                s = n % STAGES
                if n >= STAGES:
                    sp.wait_ge(v_used, used_by(c, unit_at("down", *divmod(n - STAGES, ND)) + 1))
                else:
                    sp.wait_ge(v_used, used_by(c, 0))
                if part == 0:
                    sp.wait_ge(d_x2, (c + 1) * 16)
                else:
                    before = n - ND
                    sp.wait_ge(d_pout[before % STAGES], stored_by(c, before // STAGES + 1))
                sp.dma_start(pin[:, s, :], acc_dram[c, :, m, :]).then_inc(d_pin[s], 16)

            def store_part(c, part, m):
                s, _ = down_seq(part, m)
                to = out_c if part == 2 else acc_dram
                sp.wait_ge(v_used, used_by(c, unit_at("down", part, m) + 1))
                sp.dma_start(to[c, :, m, :], pout[:, s, :]).then_inc(d_pout[s], 16)

            def units(c, scan):
                for u in range(NU):
                    if u + 1 < NU and UNITS[u + 1][0] == "down":
                        load_part(c, *UNITS[u + 1][1:])
                    if scan or u + AHEAD_LOAD < NU:
                        load_raw(c, u + AHEAD_LOAD)
                    if u and UNITS[u - 1][0] == "down":
                        store_part(c, *UNITS[u - 1][1:])
                    if u + AHEAD_SPLIT in CACHED:
                        load_lo(c, u + AHEAD_SPLIT)
                    if scan and ("sums", 1) in SCAN_AT[u]:
                        store_x2(c + 1)
                    if scan and ("norm", PAIRS) in SCAN_AT[u]:
                        load_x(c + 2)
                store_part(c, *UNITS[NU - 1][1:])

            for s in range(STAGES):
                sp.sem_inc(d_pout[s], 16)
            sp.dma_start(vec[:, 2, :], cT).then_inc(d_const, 16)
            sp.dma_start(y[:, :, :], x_c[0]).then_inc(d_x, 16)
            sp.dma_start(vec[:, 0, :], dt_bias).then_inc(d_const, 16)
            sp.dma_start(vec[:, 1, :], d_vec).then_inc(d_const, 16)
            sp.dma_start(aneg[:, :], a_log).then_inc(d_const, 16)
            sp.dma_start(identf[:, :], ident).then_inc(d_const, 16)
            sp.dma_start(xpw[:, :, :], x_proj).then_inc(d_const, 16)
            sp.dma_start(dtw[:, :], dt_proj).then_inc(d_const, 16)
            for n in range(0, MOD_BEFORE_PREP, 2):
                load_mod(sp, n)
            for i in range(NC):
                load_prep(i)
                if i:
                    store_prep(i - 1)
                if i == 3 * PAIRS - 1:
                    for n in range(MOD_BEFORE_PREP, 6 * ND, 2):
                        load_mod(sp, n)
            store_prep(NC - 1)
            for s in range(HI_SLOTS):
                sp.wait_ge(d_prep_out[s], 16 * len(range(s, NC, HI_SLOTS)))
            for u in range(RAW_SLOTS):
                load_raw(None, u)
            for u in range(RAW_SLOTS, AHEAD_LOAD):
                load_raw(0, u)
            store_x2(0)
            load_x(1)
            with sp.Fori(0, CHUNKS - 1) as c:
                units(c, True)
            units(CHUNKS - 1, False)
            sp.wait_ge(d_x2, CHUNKS * 16)
            sp.wait_ge(d_x, (CHUNKS + 1) * 16)
            for s in range(STAGES):
                sp.wait_ge(d_pout[s], stored_by(CHUNKS, 0))

        @block.tensor
        def _(pe):
            def sums(c, k, of, bank):
                for i in range(ND):
                    last = nc.tensor.matmul(bank, ones[:, :], of[:, i, :], start=(i == 0), stop=(i == ND - 1))
                last.then_inc(pe_sums, 1)

            def scan_piece(c, kind, n):
                if kind == "sums":
                    if n == 0:
                        pe.wait_ge(d_x, (c + 1) * 16)
                    else:
                        pe.wait_ge(g_add, (c + 1) * GROUPS)
                    sums(c, n, y, BC[:, 0, :])
                elif kind == "squares":
                    pe.wait_ge(a_sq, 8 * c + 4 * n + 4)
                    sums(c, n, dtb, BC[:, 1, :])
                elif kind == "project":
                    pe.wait_ge(a_h, PAIRS * (c + 1))
                    for i in range(ND):
                        last = nc.tensor.matmul(BC[:, 1, :], xpw[:, i, :], hb[:, i, :], start=(i == 0), stop=(i == ND - 1))
                    last.then_inc(pe_xp, 1)
                elif kind == "dt":
                    pe.wait_ge(a_xs, c + 1)
                    pe.wait_ge(a_sp, c * PAIRS + n)
                    for a in range(2):
                        i = 2 * n + a
                        last = nc.tensor.matmul(DA[:, a, :], dtw[:, i * P:(i + 1) * P], xdt[:, :], start=True, stop=True)
                    last.then_inc(pe_dt, 1)
                elif (kind, n) == ("states", 0) or kind == "group" and n % PAIRS == 2 and n + PAIRS < GROUPS:
                    s = 0 if kind == "states" else n // PAIRS + 1
                    if s == 0:
                        pe.wait_ge(v_xs, c + 1)
                    else:
                        pe.wait_ge(a_bc, c * NS + s)
                    for b, row in ((0, RANK + s), (1, RANK + NS + s)):
                        last = nc.tensor.matmul(BC[:, b, :], sel[:, row:row + 1].to_broadcast([P, P]), xs[:, :],
                                                start=True, stop=True)
                    last.then_inc(pe_bc, 1)

            def products(out, pairs, start=True, stop=True):
                n = len(pairs)
                for k, ((w_hi, w_lo), (x_hi, x_lo)) in enumerate(pairs):
                    for e, (w, x) in enumerate(((w_hi, x_hi), (w_hi, x_lo), (w_lo, x_hi))):
                        last = nc.tensor.matmul(out, w, x, start=(start and k == 0 and e == 0),
                                                stop=(stop and k == n - 1 and e == 2))
                return last

            def unit(c, u):
                kind, part, j = UNITS[u]
                s, bank = u % HI_SLOTS, FP[:, u % BANKS, :]
                hi, lo = whi[:, s, :], wlo[:, s, :]
                k0, k1 = PARTS[part]
                pe.wait_ge(a_hi, c * NU + u + 1)
                if u in CACHED:
                    pe.wait_ge(d_lo[u % HI_SLOTS], lo_loaded(c, u))
                else:
                    pe.wait_ge(g_lo, lo_made(c, u + 1))
                pe.wait_ge(v_used, used_by(c, max(0, u - BANKS + 1)))
                if kind == "lora_a":
                    pe.wait_ge(a_h2, PAIRS * (c + 1))
                    pe.wait_ge(g_h2, PAIRS * (c + 1))
                    last = products(FP[0:LA_COLS, u % BANKS, :], [
                        ((hi[:, k * LA_COLS:(k + 1) * LA_COLS], lo[:, k * LA_COLS:(k + 1) * LA_COLS]),
                         (xhi[:, k, :], xlo[:, k, :])) for k in range(ND)])
                elif kind in ("gate", "up"):
                    for k in range(ND):
                        at = slice(k * P, (k + 1) * P)
                        nc.tensor.matmul(bank, hi[:, at], xhi[:, k, :], start=(k == 0), stop=False)
                        nc.tensor.matmul(bank, hi[:, at], xlo[:, k, :], start=False, stop=False)
                        nc.tensor.matmul(bank, lo[:, at], xhi[:, k, :], start=False, stop=False)
                    if j == 0:
                        pe.wait_ge(v_used, used_by(c, 1))
                    nc.tensor.matmul(bank, lo[0:LA_COLS // 2, ND * P:], ts[0:LA_COLS // 2, :], start=False, stop=False)
                    last = nc.tensor.matmul(bank, hi[0:LA_COLS, ND * P:], ts[:, :], start=False, stop=True)
                else:
                    w = TD_COLS if kind == "lora_down" else P
                    if kind == "lora_down":
                        pe.wait_ge(g_hlo, split_by(c, k1 - (part == 2)))
                    pairs = [((hi[:, k * w:(k + 1) * w], lo[:, k * w:(k + 1) * w]), (hhi[:, (k0 + k) % PART_MAX, :], hlo[:, (k0 + k) % PART_MAX, :]))
                             for k in range(k1 - k0)]
                    out = FP[0:w, u % BANKS, :]
                    products(out, pairs[:-1], stop=False)
                    if part == 2 and kind == "lora_down":
                        pe.wait_ge(g_hlo, split_by(c, k1))
                    elif part == 2 and j == 0:
                        pe.wait_ge(v_hlo, c + 1)
                    last = products(out, pairs[-1:], start=False)
                last.then_inc(pe_unit, 1)

            def mods(a, b):
                for n in range(a, b):
                    pe.wait_ge(d_modw[n % MOD_SLOTS], (n // MOD_SLOTS + 1) * 16)
                    col = FP[:, n // (3 * ND), n % (3 * ND):n % (3 * ND) + 1]
                    for k in range(ND):
                        last = nc.tensor.matmul(col, modw[:, n % MOD_SLOTS, k, :], vec[:, 3, k:k + 1],
                                                start=(k == 0), stop=(k == ND - 1))
                    last.then_inc(pe_mod, 1)

            pe.sem_inc(pe_unit, 1)
            pe.wait_ge(v_const, 2)
            pe.wait_ge(d_const, N_CONST)
            pe.wait_ge(a_const, 3)
            for kind, n in PIECES_ALONE:
                if (kind, n) == ("project", 0):
                    mods(0, 3 * ND)
                if kind == "group" and n < 3 * ND:
                    mods(3 * ND + n, 3 * ND + n + 1)
                scan_piece(0, kind, n)
            pe.wait_ge(v_mod, 2)
            with pe.Fori(0, CHUNKS - 1) as c:
                for u in range(NU):
                    for kind, n in SCAN_AT[u]:
                        scan_piece(c + 1, kind, n)
                    unit(c, u)
            for u in range(NU):
                unit(CHUNKS - 1, u)

        @block.scalar
        def _(act):
            PER = 2 * 2 + PAIRS + 1

            def copy_bc(c, s):
                act.wait_ge(pe_bc, c * NS + s + 1)
                if s >= 2 or not isinstance(c, int):
                    act.wait_ge(g_add, c * GROUPS + PAIRS * max(0, s - 1))
                nc.scalar.activation(b_row[:, s % 2, :], BC[:, 0, :], ACT.Copy)
                nc.scalar.activation(c_row[:, s % 2, :], BC[:, 1, :], ACT.Copy).then_inc(a_bc, 1)

            def scan_piece(c, kind, n):
                if kind == "center":
                    q = n % PAIRS
                    act.wait_ge(v_center, 16 * c + 2 * n + 2)
                    nc.scalar.activation(pair(dtb, q), pair(hb, q), ACT.Square).then_inc(a_sq, 1)
                elif kind == "rstd":
                    at = c * PER + (2 + PAIRS) * n
                    act.wait_ge(pe_sums, 4 * c + 2 * n + 2)
                    nc.scalar.activation(tmp[0], BC[:, 1, :], ACT.Ln, scale=1.0 / D, bias=epsc[:, :]).then_inc(a_step, 1)
                    act.wait_ge(a_step, at + 1)
                    nc.scalar.activation(tmp[1], tmp[0], ACT.Exp, scale=-0.5).then_inc(a_step, 1)
                    act.wait_ge(a_step, at + 2)
                    nc.scalar.activation(tmp[2], tmp[1], ACT.Square).then_inc(a_seed, 1)
                    if isinstance(c, int) and c == 0:
                        act.wait_ge(v_mod, n + 1)
                    elif n == 1:
                        act.wait_ge(pe_unit, done_by(c - 1, LAST_UP + 1))
                elif kind == "norm":
                    n, q = divmod(n, PAIRS)
                    act.wait_ge(v_norm, 8 * c + PAIRS * n + q + 1)
                    for i in (2 * q, 2 * q + 1):
                        if n == 0:
                            last = nc.scalar.activation(hb[:, i, :], hb[:, i, :], ACT.Identity, scale=modc(CA, i), bias=modc(SA, i))
                        else:
                            last = nc.scalar.activation(xhi[:, i, :], hb[:, i, :], ACT.Identity, scale=modc(CB, i), bias=modc(SB, i))
                    if n == 0:
                        last.then_inc(a_h, 1)
                    elif q == PAIRS - 1:
                        last.then_inc(a_step, 1)
                elif kind == "h2":
                    if n == 0:
                        act.wait_ge(a_step, (c + 1) * PER)
                    for i in (2 * n, 2 * n + 1):
                        last = nc.scalar.activation(hb[:, i, :], hb[:, i, :], ACT.Identity, scale=modc(CB, i), bias=modc(SB, i))
                    last.then_inc(a_h2, 1)
                elif kind == "project":
                    act.wait_ge(pe_xp, c + 1)
                    if not (isinstance(c, int) and c == 0):
                        act.wait_ge(pe_bc, c * NS)
                        act.wait_ge(pe_dt, c * PAIRS)
                    nc.scalar.activation(xs[:, :], BC[:, 1, :], ACT.Copy)
                    nc.scalar.activation(xdt[:, :], BC[0:RANK, 1, :], ACT.Copy).then_inc(a_xs, 1)
                elif kind == "dt":
                    act.wait_ge(pe_dt, c * PAIRS + n + 1)
                    if n >= 2:
                        act.wait_ge(v_dt, c * PAIRS + n - 1)
                    for a in range(2):
                        i = 2 * n + a
                        nc.scalar.activation(ring[:, n % 2, a, :], DA[:, a, :], ACT.Abs, bias=vec[:, 0, i:i + 1])
                        e = nc.scalar.activation(dtb[:, i, :], DA[:, a, :], ACT.Relu, bias=vec[:, 0, i:i + 1])
                    e.then_inc(a_step, 1)
                    act.wait_ge(a_step, c * PER + 2 + n + 1)
                    nc.scalar.activation(ring[:, n % 2, :, :], ring[:, n % 2, :, :], ACT.Exp, scale=-1.0).then_inc(a_sp, 1)
                elif kind == "states":
                    s, q = divmod(n, PAIRS)
                    if s == 0:
                        act.wait_ge(v_dt, c * PAIRS + q + 1)
                    if n == 0:
                        copy_bc(c, 0)
                    elif q == PAIRS - 1 and s + 1 < NS:
                        copy_bc(c, s + 1)
                    for a in range(2):
                        i = 2 * q + a
                        act.wait_ge(v_scan[a], c * GROUPS + n)
                        nc.scalar.activation(DA[:, a, :], dtb[:, i, :], ACT.Exp,
                                             scale=aneg[:, i * NS + s:i * NS + s + 1]).then_inc(a_da[a], 1)

            def split_hi(c, u, first=False):
                s, r, w = u % HI_SLOTS, u % RAW_SLOTS, unit_cols(u)
                act.wait_ge(d_raw[r], 16 * (c * (NU // RAW_SLOTS) + u // RAW_SLOTS + 1))
                if not first:
                    act.wait_ge(pe_unit, done_by(c, max(0, u - HI_SLOTS + 1)))
                nc.scalar.activation(whi[:, s, 0:w], raw[:, r, 0:w], ACT.Copy).then_inc(a_hi, 1)

            def prep_hi(i):
                w = unit_cols(CACHED[i])
                act.wait_ge(d_prep[i % RAW_SLOTS], 16 * (i // RAW_SLOTS + 1))
                if i >= HI_SLOTS:
                    act.wait_ge(g_prep, i - HI_SLOTS + 1)
                nc.scalar.activation(whi[:, i % HI_SLOTS, 0:w], raw[:, i % RAW_SLOTS, 0:w], ACT.Copy).then_inc(a_prep, 1)

            def before(c, u):
                kind, part, j = UNITS[u - 1]
                bank = (u - 1) % BANKS
                if kind == "lora_a":
                    act.wait_ge(pe_unit, done_by(c, u))
                    nc.scalar.activation(ts[:, :], FP[0:LA_COLS, bank, :], ACT.Copy).then_inc(a_ls, 1)
                elif kind == "gate":
                    act.wait_ge(pe_unit, done_by(c, u))
                    act.wait_ge(g_hlo, split_by(c, max(0, j - 1)))
                    nc.scalar.activation(hid[:, j % 2, :], FP[:, bank, :], ACT.Tanh, scale=0.5).then_inc(a_th, 1)

            def after(c, u):
                kind, part, j = UNITS[u - 1]
                if kind == "up":
                    act.wait_ge(v_used, used_by(c, u))
                    nc.scalar.activation(hhi[:, j % PART_MAX, :], hid[:, j % 2, :], ACT.Copy).then_inc(a_hh, 1)
                elif kind == "lora_down" and part == 2:
                    act.wait_ge(v_used, used_by(c, u))
                    at = slice(LORA_AT, LORA_AT + LORA)
                    nc.scalar.activation(hhi[at, (NH - 1) % PART_MAX, :], hid[at, NH % 2, :], ACT.Copy).then_inc(a_hh, 1)

            act.wait_ge(d_const, N_CONST)
            act.wait_ge(v_const, 1)
            nc.scalar.activation(small[:, 0, :], vec[:, 2, :], ACT.Tanh, scale=0.5).then_inc(a_const, 1)
            nc.scalar.activation(aneg[:, :], aneg[:, :], ACT.Exp).then_inc(a_const, 1)
            nc.scalar.activation(sel[:, :], identf[:, :], ACT.Copy).then_inc(a_const, 1)
            for kind, n in PIECES_ALONE:
                scan_piece(0, kind, n)
                for i in PREP_AT.get((kind, n), []):
                    prep_hi(i)
                if (kind, n) == START_AT:
                    act.wait_ge(g_prep, NC)
                    for u in range(AHEAD_SPLIT):
                        split_hi(0, u, first=True)
            with act.Fori(0, CHUNKS - 1) as c:
                for u in range(NU):
                    if u:
                        before(c, u)
                    split_hi(c, u + AHEAD_SPLIT)
                    for kind, n in SCAN_AT[u]:
                        scan_piece(c + 1, kind, n)
                    if u:
                        after(c, u)
            for u in range(NU):
                if u:
                    before(CHUNKS - 1, u)
                if u + AHEAD_SPLIT < NU:
                    split_hi(CHUNKS - 1, u + AHEAD_SPLIT)
                if u:
                    after(CHUNKS - 1, u)

        @block.vector
        def _(dve):
            PER = 2 * 3 + PAIRS * (len(LOG1P) + 1)
            V = nc.vector

            def dbx(c, g):
                s, q = divmod(g, PAIRS)
                if q == 0:
                    dve.wait_ge(a_bc, c * NS + s + 1)
                if g >= 3:
                    dve.wait_ge(g_add, c * GROUPS + g - 2)
                V.tensor_tensor(ring[:, g % 3, :, :], pair(hb, q), over_pair(b_row[:, s % 2, :]), ALU.mult).then_inc(v_dbx, 1)

            def scan_piece(c, kind, n):
                if kind == "center":
                    ln, q = divmod(n, PAIRS)
                    if q == 0:
                        dve.wait_ge(pe_sums, 4 * c + 2 * ln + 1)
                        if ln == 0 and not (isinstance(c, int) and c == 0):
                            dve.wait_ge(g_h2, PAIRS * c)
                    V.scalar_tensor_tensor(out=pair(hb, q), in0=over_pair(BC[:, 0, :]), scalar=-1.0 / D,
                                           in1=pair(y, q), op0=ALU.mult, op1=ALU.add).then_inc(v_center, 2)
                elif kind == "rstd":
                    at = c * PER + (3 + PAIRS * (len(LOG1P) + 1)) * n
                    dve.wait_ge(a_seed, 2 * c + n + 1)
                    V.tensor_scalar(tmp[3], BC[:, 1, :], 1.0 / D, EPS, ALU.mult, ALU.add).then_inc(v_step, 1)
                    dve.wait_ge(v_step, at + 1)
                    V.scalar_tensor_tensor(out=tmp[3], in0=tmp[3], scalar=-0.5, in1=tmp[2], op0=ALU.mult, op1=ALU.mult).then_inc(v_step, 1)
                    dve.wait_ge(v_step, at + 2)
                    V.scalar_tensor_tensor(out=tmp[0], in0=tmp[3], scalar=1.5, in1=tmp[1], op0=ALU.add, op1=ALU.mult).then_inc(v_step, 1)
                    dve.wait_ge(v_step, at + 3)
                elif kind == "norm":
                    q = n % PAIRS
                    V.tensor_tensor(pair(hb, q), pair(hb, q), over_pair(tmp[0]), ALU.mult).then_inc(v_norm, 1)
                elif kind == "start":
                    for i in range(n * PAIRS, (n + 1) * PAIRS):
                        if i % 2 == 0:
                            dve.wait_ge(a_h, PAIRS * c + i // 2 + 1)
                        last = V.scalar_tensor_tensor(out=y[:, i, :], in0=hb[:, i, :], scalar=gad[:, i:i + 1], in1=y[:, i, :],
                                                      op0=ALU.mult, op1=ALU.add)
                    last.then_inc(v_yinit, 1)
                elif kind == "split":
                    dve.wait_ge(a_xs, c + 1)
                    V.tensor_tensor(xs[64:128, :], BC[64:128, 1, :], xs[64:128, :].bitcast(F32), ALU.subtract).then_inc(v_xs, 1)
                elif kind == "poly":
                    n, k0 = divmod(n, POLY)
                    at = c * PER + 3 + n * (len(LOG1P) + 1)
                    e, poly = ring[:, n % 2, :, :], ring[:, 2, :, :]
                    steps = len(LOG1P) // POLY
                    if k0 == 0:
                        dve.wait_ge(a_sp, c * PAIRS + n + 1)
                    for k in range(k0 * steps, (k0 + 1) * steps):
                        if k == 0:
                            V.tensor_scalar(poly, e, LOG1P[-1], None, ALU.mult).then_inc(v_step, 1)
                        else:
                            dve.wait_ge(v_step, at + k)
                            V.scalar_tensor_tensor(out=poly, in0=poly, scalar=LOG1P[-1 - k], in1=e, op0=ALU.add, op1=ALU.mult).then_inc(v_step, 1)
                elif kind == "u":
                    at = c * PER + 3 + n * (len(LOG1P) + 1) + len(LOG1P)
                    dve.wait_ge(v_step, at)
                    V.tensor_tensor(pair(dtb, n), pair(dtb, n), ring[:, 2, :, :], ALU.add).then_inc(v_step, 1)
                    dve.wait_ge(v_step, at + 1)
                    if n == 0:
                        dve.wait_ge(v_yinit, 2 * (c + 1))
                    for i in (2 * n, 2 * n + 1):
                        last = V.scalar_tensor_tensor(out=hb[:, i, :], in0=dtb[:, i, :], scalar=modc(GA, i), in1=hb[:, i, :],
                                                      op0=ALU.mult, op1=ALU.mult)
                    last.then_inc(v_dt, 1)
                elif kind == "states":
                    s, q = divmod(n, PAIRS)
                    if n == 0:
                        dve.wait_ge(v_dt, (c + 1) * PAIRS)
                        dbx(c, 0)
                    buf = ring[:, n % 3, :, :]
                    dve.wait_ge(v_dbx, c * GROUPS + n + 1)
                    for a in range(2):
                        i = 2 * q + a
                        dve.wait_ge(a_da[a], c * GROUPS + n + 1)
                        initial = 0.0 if isinstance(c, int) and c == 0 else hst[:, s * ND + i:s * ND + i + 1]
                        V.tensor_tensor_scan(buf[:, a, :], DA[:, a, :], buf[:, a, :], initial, ALU.mult, ALU.add).then_inc(v_scan[a], 1)
                elif kind == "group":
                    s, q = divmod(n, PAIRS)
                    buf = ring[:, n % 3, :, :]
                    if n + 1 < GROUPS:
                        dbx(c, n + 1)
                    for a in range(2):
                        dve.wait_ge(v_scan[a], c * GROUPS + n + 1)
                    V.tensor_copy(hst[:, s * ND + 2 * q:s * ND + 2 * q + 2], buf[:, :, T - 1]).then_inc(v_save, 1)
                    if n in POOL_GROUPS:
                        return
                    dve.wait_ge(v_save, c * GROUPS + n + 1)
                    V.tensor_tensor(buf, buf, over_pair(c_row[:, s % 2, :]), ALU.mult).then_inc(v_hc, 1)

            def used(c, u):
                kind, part, j = UNITS[u - 1]
                bank = (u - 1) % BANKS
                h = hid[:, j % 2, :]
                if kind == "lora_a":
                    dve.wait_ge(a_ls, c + 1)
                    V.tensor_tensor(ts[32:64, :], FP[32:64, bank, :], ts[32:64, :].bitcast(F32), ALU.subtract).then_inc(v_used, 1)
                elif kind == "gate":
                    dve.wait_ge(a_th, c * NH + j + 1)
                    V.scalar_tensor_tensor(out=h, in0=h, scalar=1.0, in1=FP[:, bank, :], op0=ALU.add, op1=ALU.mult).then_inc(v_used, 1)
                elif kind == "up":
                    dve.wait_ge(pe_unit, done_by(c, u))
                    dve.wait_ge(v_used, used_by(c, u - 1))
                    V.scalar_tensor_tensor(out=h, in0=h, scalar=0.5, in1=FP[:, bank, :], op0=ALU.mult, op1=ALU.mult).then_inc(v_used, 1)
                elif kind == "lora_down":
                    at = slice(LORA_AT, LORA_AT + LORA)
                    dve.wait_ge(pe_unit, done_by(c, u))
                    if part == 0:
                        V.tensor_copy(tda[at, :], FP[at, bank, :]).then_inc(v_used, 1)
                    elif part == 1:
                        V.tensor_tensor(tda[at, :], FP[at, bank, :], tda[at, :], ALU.add).then_inc(v_used, 1)
                    else:
                        dve.wait_ge(g_hlo, split_by(c, NH - 1))
                        V.tensor_tensor(hid[at, NH % 2, :], FP[at, bank, :], tda[at, :], ALU.add).then_inc(v_used, 1)
                else:
                    if (part, j) == (2, 0):
                        dve.wait_ge(a_hh, (c + 1) * N_HID)
                        at, k = slice(LORA_AT, LORA_AT + LORA), (NH - 1) % PART_MAX
                        V.tensor_tensor(hlo[at, k, :], hid[at, NH % 2, :], hhi[at, k, :].bitcast(F32), ALU.subtract).then_inc(v_hlo, 1)
                    s, k = down_seq(part, j)
                    dve.wait_ge(pe_unit, done_by(c, u))
                    dve.wait_ge(d_pin[s], (c * PER_STAGE + k + 1) * 16)
                    dve.wait_ge(d_pout[s], stored_by(c, k))
                    V.scalar_tensor_tensor(out=pout[:, s, :], in0=FP[:, bank, :], scalar=modc(GB, j), in1=pin[:, s, :],
                                           op0=ALU.mult, op1=ALU.add).then_inc(v_used, 1)

            def mod_vectors():
                n = [0]

                def then(ins):
                    n[0] += 1
                    ins.then_inc(v_const, 1)
                    dve.wait_ge(v_const, 2 + n[0])

                def away_from_zero(v):
                    then(V.tensor_scalar(small[:, 0, :], v, 0.0, 2.0, ALU.is_ge, ALU.mult))
                    then(V.scalar_tensor_tensor(out=small[:, 1, :], in0=v, scalar=-1.0, in1=v, op0=ALU.mult, op1=ALU.max))
                    then(V.tensor_scalar(small[:, 1, :], small[:, 1, :], 0.25, None, ALU.max))
                    then(V.scalar_tensor_tensor(out=v, in0=small[:, 0, :], scalar=-1.0, in1=small[:, 1, :], op0=ALU.add, op1=ALU.mult))

                def first():
                    dve.wait_ge(pe_mod, 3 * ND)
                    then(V.tensor_copy(mod[:, 0:3, :], FP[:, 0, 0:3 * ND].rearrange("p (a b) -> p a b", a=3)))
                    then(V.tensor_scalar(mod[:, CA, :], mod[:, CA, :], 1.0, None, ALU.add))
                    away_from_zero(mod[:, GA, :])
                    dve.wait_ge(a_const, 2)
                    then(V.tensor_scalar(aneg[:, :], aneg[:, :], -1.0, None, ALU.mult))
                    V.tensor_tensor(gad[:, :], mod[:, GA, :], vec[:, 1, :], ALU.mult).then_inc(v_mod, 1)
                    dve.wait_ge(v_mod, 1)

                def second():
                    dve.wait_ge(pe_mod, 6 * ND)
                    then(V.tensor_copy(mod[:, 3:6, :], FP[:, 1, 0:3 * ND].rearrange("p (a b) -> p a b", a=3)))
                    then(V.tensor_scalar(mod[:, CB, :], mod[:, CB, :], 1.0, None, ALU.add))
                    away_from_zero(mod[:, GB, :])
                    V.tensor_copy(small[:, 0, :], mod[:, GB, :]).then_inc(v_mod, 1)
                return first, second

            dve.sem_inc(v_used, 1)
            V.memset(ones[:, :], 1.0)
            V.memset(epsc[:, :], EPS).then_inc(v_const, 1)
            dve.wait_ge(d_const, N_CONST)
            dve.wait_ge(a_const, 1)
            V.scalar_tensor_tensor(out=small[:, 0, :], in0=small[:, 0, :], scalar=1.0, in1=vec[:, 2, :],
                                   op0=ALU.add, op1=ALU.mult).then_inc(v_c, 1)
            dve.wait_ge(v_c, 1)
            V.tensor_scalar(vec[:, 3, :], small[:, 0, :], 0.5, None, ALU.mult).then_inc(v_const, 1)
            mod_first, mod_second = mod_vectors()
            for kind, n in PIECES_ALONE:
                if (kind, n) == ("start", 0):
                    mod_first()
                scan_piece(0, kind, n)
                if (kind, n) == ("group", 7 * PAIRS):
                    mod_second()
            with dve.Fori(0, CHUNKS - 1) as c:
                for u in range(NU):
                    if u:
                        used(c, u)
                    for kind, n in SCAN_AT[u]:
                        scan_piece(c + 1, kind, n)
                used(c, NU)
            for u in range(1, NU + 1):
                used(CHUNKS - 1, u)

        @block.gpsimd
        def _(pool):
            G = nc.gpsimd

            def scan_piece(c, kind, n):
                if kind == "group":
                    q = n % PAIRS
                    if n in POOL_GROUPS:
                        buf = ring[:, n % 3, :, :]
                        pool.wait_ge(v_save, c * GROUPS + n + 1)
                        G.tensor_tensor(buf, buf, over_pair(c_row[:, n // PAIRS % 2, :]), ALU.mult).then_inc(g_hc, 1)
                        pool.wait_ge(g_hc, c * len(POOL_GROUPS) + POOL_GROUPS.index(n) + 1)
                    else:
                        pool.wait_ge(v_hc, c * (GROUPS - len(POOL_GROUPS)) + sum(k not in POOL_GROUPS for k in range(n + 1)))
                    if n >= PAIRS:
                        pool.wait_ge(g_add, c * GROUPS + n - PAIRS + 1)
                    G.tensor_tensor(pair(y, q), pair(y, q), ring[:, n % 3, :, :], ALU.add).then_inc(g_add, 1)
                elif kind == "h2":
                    pool.wait_ge(a_h2, PAIRS * c + n + 1)
                    G.tensor_tensor(pair(xlo, n), pair(hb, n), pair(xhi, n).bitcast(F32), ALU.subtract).then_inc(g_h2, 1)

            def prep_lo(i):
                s, w = i % HI_SLOTS, unit_cols(CACHED[i])
                pool.wait_ge(a_prep, i + 1)
                if i >= HI_SLOTS:
                    pool.wait_ge(d_prep_out[s], 16 * (i // HI_SLOTS))
                G.tensor_tensor(wlo[:, s, 0:w], raw[:, i % RAW_SLOTS, 0:w], whi[:, s, 0:w].bitcast(F32), ALU.subtract).then_inc(g_prep, 1)

            def split_lo(c, u):
                if u in CACHED:
                    return
                s, r, w = u % HI_SLOTS, u % RAW_SLOTS, unit_cols(u)
                pool.wait_ge(a_hi, c * NU + u + 1)
                G.tensor_tensor(wlo[:, s, 0:w], raw[:, r, 0:w], whi[:, s, 0:w].bitcast(F32), ALU.subtract).then_inc(g_lo, 1)

            def after(c, u):
                kind, part, j = UNITS[u - 1]
                if kind == "up":
                    pool.wait_ge(a_hh, c * N_HID + j + 1)
                    k = j % PART_MAX
                    G.tensor_tensor(hlo[:, k, :], hid[:, j % 2, :], hhi[:, k, :].bitcast(F32), ALU.subtract).then_inc(g_hlo, 1)

            for n in range(1, MOD_BEFORE_PREP, 2):
                load_mod(pool, n)
            pool.sem_inc(g_hlo, 1)
            for kind, n in PIECES_ALONE:
                scan_piece(0, kind, n)
                if (kind, n) == ("group", 10):
                    for k in range(MOD_BEFORE_PREP + 1, 6 * ND, 2):
                        load_mod(pool, k)
                for i in PREP_AT.get((kind, n), []):
                    prep_lo(i)
                if (kind, n) == START_AT:
                    for s in range(HI_SLOTS):
                        pool.wait_ge(d_prep_out[s], 16 * len(range(s, NC, HI_SLOTS)))
                    for u in range(AHEAD_SPLIT):
                        split_lo(0, u)
            with pool.Fori(0, CHUNKS - 1) as c:
                for u in range(NU):
                    split_lo(c, u + AHEAD_SPLIT)
                    for kind, n in SCAN_AT[u]:
                        scan_piece(c + 1, kind, n)
                    if u:
                        after(c, u)
            for u in range(NU):
                if u + AHEAD_SPLIT < NU:
                    split_lo(CHUNKS - 1, u + AHEAD_SPLIT)
                if u:
                    after(CHUNKS - 1, u)


LAST_UP = max(u for u, unit in enumerate(UNITS) if unit[0] == "up")


def layout(L0_attn_x, L0_attn_A_log, L0_attn_D, L0_attn_x_proj_w, L0_attn_dt_proj_w, L0_attn_dt_proj_b,
           L0_ffn_gate_w, L0_ffn_up_w, L0_ffn_down_w, L0_ffn_gate_a, L0_ffn_gate_b, L0_ffn_up_a, L0_ffn_up_b,
           L0_ffn_down_a, L0_ffn_down_b, L0_c, L0_wmod):
    import numpy as np

    def columns(v):
        return v.reshape(ND, P).T

    def blocks(w, rows):
        padded = np.zeros((rows, w.shape[1]), w.dtype)
        padded[:w.shape[0]] = w
        return padded.reshape(rows, w.shape[1] // P, P).transpose(2, 1, 0)

    f = np.float32
    wm = L0_wmod.reshape(ND, P, 6, ND, P)[:, :, MOD_ORDER].transpose(2, 3, 1, 0, 4).reshape(6 * ND, P, ND, P)
    xp = np.concatenate([blocks(L0_attn_x_proj_w, 64)] * 2, axis=2)
    w_la = np.concatenate([blocks(L0_ffn_gate_a, LORA), blocks(L0_ffn_up_a, LORA)] * 2, axis=2).reshape(P, ND * LA_COLS)
    w_gu = np.zeros((NH, 2, P, ND + 1, P), f)
    for n, (w, b) in enumerate(((L0_ffn_gate_w, L0_ffn_gate_b), (L0_ffn_up_w, L0_ffn_up_b))):
        w_gu[:, n, :, 0:ND, :] = blocks(w, NH * P).reshape(P, ND, NH, P).transpose(2, 0, 1, 3)
        padded = np.zeros((NH * P, LORA), f)
        padded[:HID] = b
        b_rows = padded.reshape(NH, P, LORA).transpose(0, 2, 1)
        for r in range(2):
            at = r * 2 * LORA + n * LORA
            w_gu[:, n, at:at + LORA, ND, :] = b_rows
    down = np.zeros((D, NH * P), f)
    down[:, :HID] = L0_ffn_down_w
    down[:, HID:HID + LORA] = L0_ffn_down_b
    w_dn = down.reshape(ND, P, NH, P).transpose(0, 3, 2, 1)
    down_a = np.zeros((TD_COLS, NH * P), f)
    down_a[LORA_AT:, :HID] = L0_ffn_down_a
    w_td = down_a.reshape(TD_COLS, NH, P).transpose(2, 1, 0)
    return {
        "x_c": np.concatenate([L0_attn_x[0].reshape(CHUNKS, T, ND, P).transpose(0, 3, 2, 1), np.zeros((1, P, ND, T), f)]), "mod_w": wm, "cT": columns(L0_c[0]), "ident": np.concatenate([np.eye(64, dtype=f)] * 2),
        "x_proj": xp, "dt_proj": L0_attn_dt_proj_w.T, "dt_bias": columns(L0_attn_dt_proj_b),
        "a_log": L0_attn_A_log.reshape(ND, P, NS).transpose(1, 0, 2).reshape(P, ND * NS), "d_vec": columns(L0_attn_D),
        "w_la": w_la, "w_gu": w_gu.reshape(NH, 2, P, GU_COLS), "w_td": w_td, "w_dn": w_dn,
    }


def kernel(**inputs):
    import numpy as np
    import concourse.bacc as bacc
    from concourse.bass_utils import run_bass_kernel_spmd

    nc = bacc.Bacc("TRN2", target_bir_lowering=False, num_devices=1)
    arrays = {n: np.ascontiguousarray(a) for n, a in layout(**{k: np.asarray(v) for k, v in inputs.items()}).items()}
    args = {n: nc.dram_tensor(n, a.shape, F32, kind="ExternalInput").ap() for n, a in arrays.items()}
    out_c = nc.dram_tensor("out_c", (CHUNKS, P, ND, T), F32, kind="ExternalOutput").ap()
    build(nc, **args, out_c=out_c)
    r = run_bass_kernel_spmd(nc, [arrays], core_ids=[0])
    return np.ascontiguousarray(r.results[0]["out_c"].transpose(0, 3, 2, 1)).reshape(1, TOKENS, D)
```
